# Optimizing a Trainium2 kernel written in Bass

```python
import numpy as np
import jax
import jax.numpy as jnp

def _softmax(x, axis=-1):
    return jax.nn.softmax(x, axis=axis)

def _gelu(x):
    return jax.nn.gelu(x, approximate=True)

def _silu(x):
    return jax.nn.silu(x)

def _sigmoid(x):
    return jax.nn.sigmoid(x)

def _layernorm(x, axis=-1, eps=1e-05):
    m = jnp.mean(x, axis=axis, keepdims=True)
    v = jnp.var(x, axis=axis, keepdims=True)
    return (x - m) / jnp.sqrt(v + eps)

def _scatter_add(tgt, idx, src, axis=0):
    return tgt.at[idx].add(src)

def _segment_sum(src, seg, n):
    return jax.ops.segment_sum(src, seg, n)
kernel_name = 'mk_gnn_ffn_d1_gnn_r8_dfbb2b'

def setup_inputs(seed: int=0):
    np.random.seed(seed)
    _w = jnp.asarray

    def _rec_inputs():
        import jax
        import jax.numpy as jnp
        _gk = jax.random.key(seed)
        x = -0.0003713 + 1 * jax.random.normal(jax.random.fold_in(_gk, 1), (6250, 256), jnp.float32)
        src = jax.random.randint(jax.random.fold_in(_gk, 2), (100000,), 0, 6250, jnp.int32)
        dst = jnp.minimum((6250 * jax.random.uniform(jax.random.fold_in(_gk, 3), (100000,)) ** 2.0).astype(jnp.int32), 49999)
        _o = jnp.argsort(dst, stable=True)
        src = src[_o]
        dst = dst[_o]
        return (x, src, dst)
    x, src, dst = _rec_inputs()

    def _L0_gnn_setup():
        import jax, jax.numpy as jnp
        import numpy as np
        N, IN_CH, HEADS, OUT_CH, E = (6250, 256, 4, 64, 100000)
        key = jax.random.key(seed)
        k1, k2, k3, k4, k5 = jax.random.split(key, 5)
        x = jax.random.normal(k1, (N, IN_CH), dtype=jnp.float32)
        edge_index = jax.random.randint(k2, (2, E), 0, N, dtype=jnp.int64)
        bw = float(np.sqrt(6.0 / (IN_CH + HEADS * OUT_CH)))
        ba = float(np.sqrt(6.0 / (HEADS + OUT_CH)))
        weight = jax.random.uniform(k3, (IN_CH, HEADS * OUT_CH), jnp.float32, -bw, bw)
        attn_l = jax.random.uniform(k4, (HEADS, OUT_CH), jnp.float32, -ba, ba)
        attn_r = jax.random.uniform(k5, (HEADS, OUT_CH), jnp.float32, -ba, ba)
        return {'x': x, 'edge_index': edge_index, 'weight': weight, 'attn_l': attn_l, 'attn_r': attn_r}
    _L0_gnn_all = _L0_gnn_setup()
    _L0_gnn_in = {k: v for k, v in _L0_gnn_all.items() if k in ('weight', 'attn_l', 'attn_r')}
    del _L0_gnn_all

    def _L0_ffn_setup():
        import jax, jax.numpy as jnp
        import numpy as np
        NUM_EXPERTS = 8
        TOP_K = 2
        B, S, D = (8, 1024, 256)

        def _moe(tokens, router_w, w1, b1, w2, b2):
            N = tokens.shape[0]
            E = router_w.shape[0]
            logits = tokens.astype(jnp.float32) @ router_w.astype(jnp.float32).T
            probs = jax.nn.softmax(logits, axis=-1)
            rw, re = jax.lax.top_k(probs, TOP_K)
            if TOP_K > 1:
                rw = rw / jnp.maximum(rw.sum(-1, keepdims=True), 1e-12)
            rw = rw.astype(tokens.dtype)
            combine = jnp.zeros((N, E), tokens.dtype).at[jnp.arange(N)[:, None], re].set(rw)
            out = tokens
            for e in range(E):
                h = jax.nn.gelu(tokens @ w1[e] + b1[e], approximate=False)
                y = h @ w2[e] + b2[e]
                out = out + combine[:, e:e + 1] * y
            return out
        key = jax.random.key(seed)
        ks = jax.random.split(key, 4)
        scale = 1.0 / np.sqrt(D).astype(np.float32)
        return {'input_embeddings': jax.random.normal(ks[0], (B, S, D), jnp.float32), 'router_w': jax.random.normal(ks[1], (NUM_EXPERTS, D), jnp.float32) * scale, 'w1': jax.random.normal(ks[2], (NUM_EXPERTS, D, D), jnp.float32) * scale, 'b1': jnp.zeros((NUM_EXPERTS, D), jnp.float32), 'w2': jax.random.normal(ks[3], (NUM_EXPERTS, D, D), jnp.float32) * scale, 'b2': jnp.zeros((NUM_EXPERTS, D), jnp.float32)}
    _L0_ffn_all = _L0_ffn_setup()
    _L0_ffn_in = {k: v for k, v in _L0_ffn_all.items() if k in ('router_w', 'w1', 'b1', 'w2', 'b2')}
    del _L0_ffn_all
    return {'x': x, 'src': src, 'dst': dst, 'L0_gnn_weight': _L0_gnn_in['weight'], 'L0_gnn_attn_l': _L0_gnn_in['attn_l'], 'L0_gnn_attn_r': _L0_gnn_in['attn_r'], 'L0_ffn_router_w': _L0_ffn_in['router_w'], 'L0_ffn_w1': _L0_ffn_in['w1'], 'L0_ffn_b1': _L0_ffn_in['b1'], 'L0_ffn_w2': _L0_ffn_in['w2'], 'L0_ffn_b2': _L0_ffn_in['b2']}

def reference(x, src, dst, L0_gnn_weight, L0_gnn_attn_l, L0_gnn_attn_r, L0_ffn_router_w, L0_ffn_w1, L0_ffn_b1, L0_ffn_w2, L0_ffn_b2):
    import jax
    import jax.numpy as jnp

    def _L0_gnn_ref(x, edge_index, weight, attn_l, attn_r):
        import jax, jax.numpy as jnp
        import numpy as np
        N, IN_CH, HEADS, OUT_CH, E = (6250, 256, 4, 64, 100000)
        heads, out_ch = attn_l.shape
        n = x.shape[0]
        xt = jnp.matmul(x, weight).reshape(-1, heads, out_ch)
        row, col = (edge_index[0], edge_index[1])
        alpha_l = jnp.einsum('ehd,hd->eh', xt[row], attn_l)
        alpha_r = jnp.einsum('ehd,hd->eh', xt[col], attn_r)
        alpha = jax.nn.softmax(jax.nn.leaky_relu(alpha_l + alpha_r, 0.01), axis=1)
        tmp = jnp.einsum('nh,nhd->nd', alpha[:n], xt[col[:n]])
        out = jnp.broadcast_to(tmp[:, None, :], (n, heads, out_ch))
        return out.reshape(n, heads * out_ch)

    def _L0_ffn_ref(input_embeddings, router_w, w1, b1, w2, b2):
        import jax, jax.numpy as jnp
        import numpy as np
        NUM_EXPERTS = 8
        TOP_K = 2
        B, S, D = (8, 1024, 256)

        def _moe(tokens, router_w, w1, b1, w2, b2):
            N = tokens.shape[0]
            E = router_w.shape[0]
            logits = tokens.astype(jnp.float32) @ router_w.astype(jnp.float32).T
            probs = jax.nn.softmax(logits, axis=-1)
            rw, re = jax.lax.top_k(probs, TOP_K)
            if TOP_K > 1:
                rw = rw / jnp.maximum(rw.sum(-1, keepdims=True), 1e-12)
            rw = rw.astype(tokens.dtype)
            combine = jnp.zeros((N, E), tokens.dtype).at[jnp.arange(N)[:, None], re].set(rw)
            out = tokens
            for e in range(E):
                h = jax.nn.gelu(tokens @ w1[e] + b1[e], approximate=False)
                y = h @ w2[e] + b2[e]
                out = out + combine[:, e:e + 1] * y
            return out
        b, s, d = input_embeddings.shape
        tokens = input_embeddings.reshape(b * s, d)
        return _moe(tokens, router_w, w1, b1, w2, b2).reshape(b, s, d)
    edge_index = jnp.stack([src, dst])
    x = x + _L0_gnn_ref(_layernorm(x, axis=-1), edge_index, L0_gnn_weight, L0_gnn_attn_l, L0_gnn_attn_r)
    x = x + _L0_ffn_ref(_layernorm(x, axis=-1)[None], L0_ffn_router_w, L0_ffn_w1, L0_ffn_b1, L0_ffn_w2, L0_ffn_b2)[0]
    return x

_drawn_inputs = setup_inputs


def setup_inputs(seed=0):
    import zlib

    import numpy as np

    out = dict(_drawn_inputs(seed))
    spreads = {'L0_ffn_b1': (0.0, 0.353), 'L0_ffn_b2': (0.0, 0.1)}
    factors = {}
    for name, (base, spread) in spreads.items():
        noise = np.random.default_rng([zlib.crc32(name.encode()), seed]).standard_normal(out[name].shape)
        drawn = base * np.exp(spread * noise) if base else spread * noise
        out[name] = jnp.asarray(drawn.astype(out[name].dtype))
    for name, factor in factors.items():
        out[name] = (out[name] * factor).astype(out[name].dtype)
    return out
```

```python
import concourse.bass as bass
from concourse import mybir
from contextlib import ExitStack

N, D, H, C, E, TOP_K = 6250, 256, 4, 64, 8, 2
P = 128
KT = D // P
GT = 4
GROUP = GT * P
FULL = N // GROUP
TILES = -(-N // P)
TAIL_ROWS = N - FULL * GROUP
STEPS = FULL + 1
ROW = D + 2 * H
EPS = 1e-5
SLOPE = 0.01
SPLIT = 64.0
UNSPLIT = 1.0 / (SPLIT * SPLIT)
HALVES = 2
USES = 2 * (E + 1)
RING_H = 4
H_WORDS = RING_H * HALVES * GROUP
LAG = 2

assert TAIL_ROWS <= P and TILES == FULL * GT + 1 and FULL % 2 == 0


def build(nc, x, src, dst, weight, attn_l, attn_r, router_w, w1, b1, w2, b2, out):
    fp32, fp16 = mybir.dt.float32, mybir.dt.float16
    i32, u32 = mybir.dt.int32, mybir.dt.uint32
    ALU = mybir.AluOpType
    ACT = mybir.ActivationFunctionType
    X = mybir.AxisListType.X

    table = nc.dram_tensor("xt_table", (N, ROW), fp32, kind="Internal").ap()
    al_table = nc.dram_tensor("al_table", (N, H), fp32, kind="Internal").ap()

    ctx = ExitStack()
    with ctx:
        def sb(name, shape, dt=fp32):
            return ctx.enter_context(nc.sbuf_tensor(name, shape, dt))

        def sem(name):
            return ctx.enter_context(nc.semaphore(name))

        def pair(name):
            return [sem(f"{name}{i}") for i in range(2)]

        bank = [ctx.enter_context(nc.psum_tensor(f"bank{i}", [P, 512], fp32)) for i in range(8)]

        ident = sb("ident", [P, P])
        ident16 = sb("ident16", [P, P], fp16)
        iota8 = sb("iota8", [P, E])
        minus_half = sb("minus_half", [P, GT])
        wext = sb("wext", [P, KT, ROW])
        attn = sb("attn", [P, 2, H, C])
        attn_prod = sb("attn_prod", [P, H, C])
        rows_in = sb("rows_in", [TILES, 2, P], i32)
        rows_f = sb("rows_f", [TILES, 2, P])
        index = sb("index", [P, 2, TILES], u32)
        index_now = sb("index_now", [P, 2, 2, GT], u32)
        router_in = sb("router_in", [E, D])
        router64 = sb("router64", [P, KT, E])
        router_hi = sb("router_hi", [P, KT, E], fp16)
        router_lo = sb("router_lo", [P, KT, E], fp16)
        b1_in = sb("b1_in", [E * HALVES, P])
        b1_col = sb("b1_col", [P, E * HALVES])
        b2_in = sb("b2_in", [96, D])
        b2_hi = sb("b2_hi", [96, D], fp16)
        b2_parts = sb("b2_parts", [96, D], fp16)
        w_in = [sb(f"w{n}_in", [P, E, KT, D]) for n in (1, 2)]
        w_hi = [sb(f"w{n}_hi", [P, E, KT, D], fp16) for n in (1, 2)]
        w_lo = [sb(f"w{n}_lo", [P, E, KT, D], fp16) for n in (1, 2)]
        x_all = sb("x_all", [P, TILES, D])
        stats = sb("stats", [P, GT, 6])
        mean_var = sb("mean_var", [P, GT, 2])
        var_eps = sb("var_eps", [P, GT])
        rstd_0 = sb("rstd_0", [P, GT])
        newton = sb("newton", [P, GT])
        rstd = sb("rstd", [P, GT])
        x0 = sb("x0", [P, 2, GT, D])
        x0T = sb("x0T", [P, 2, KT, GROUP])
        xt_out = sb("xt_out", [P, 2, GT, ROW])
        xg = sb("xg", [P, 2, GT, ROW])
        alg = sb("alg", [P, 2, GT, H])
        score = sb("score", [P, GT, H])
        lrelu = sb("lrelu", [P, GT, H])
        top = sb("top", [P, GT])
        shifted = sb("shifted", [P, GT, H])
        expo = sb("expo", [P, GT, H])
        total = sb("total", [P, GT])
        inverse = sb("inverse", [P, GT])
        alpha = sb("alpha", [P, GT, H])
        prod = sb("prod", [P, GT, H, C])
        tmp = sb("tmp", [P, GT, C])
        x2 = sb("x2", [P, GT, D])
        x2T_hi = sb("x2T_hi", [P, 2, KT, GROUP], fp16)
        x2T_lo = sb("x2T_lo", [P, 2, KT, GROUP], fp16)
        logits = sb("logits", [P, GT, E])
        logit_top = sb("logit_top", [P, GT])
        logit_shifted = sb("logit_shifted", [P, GT, E])
        logit_exp = sb("logit_exp", [P, GT, E])
        prob_total = sb("prob_total", [P, GT])
        prob_inverse = sb("prob_inverse", [P, GT])
        prob = sb("prob", [P, GT, E])
        best = sb("best", [P, GT, 8])
        best_index = sb("best_index", [P, GT, 8], u32)
        best_f = sb("best_f", [P, GT, TOP_K])
        mask = sb("mask", [P, 2, GT, E])
        kept = sb("kept", [P, GT, E])
        comb = sb("comb", [P, 2, GT, E])
        comb64 = sb("comb64", [P, GT, E])
        comb_parts = sb("comb_parts", [P, GT, 96], fp16)
        combT = sb("combT", [96, 2, GROUP], fp16)
        acc = sb("acc", [P, 2, GT, D])
        h32 = sb("h32", [P, 2, HALVES, GROUP])
        h_hi, h_lo = [w_in[0][:].rearrange("p e k n -> p (e k n)").bitcast(fp16)[:, n * H_WORDS:(n + 1) * H_WORDS].rearrange(
            "p (r f n) -> p r f n", r=RING_H, f=HALVES) for n in range(2)]

        s_settled = sem("waits_settled")
        s_w = sem("gnn_weights_loaded")
        s_small = sem("small_inputs_loaded")
        s_experts = sem("expert_weights_loaded")
        s_const = sem("constants_made")
        s_rows_f = sem("edge_rows_as_float")
        s_setup_tr = sem("setup_transposed")
        s_setup = sem("setup_evacuated")
        s_wext = sem("wext_made")
        s_experts_split = sem("expert_weights_split")
        setup_chain = sem("setup_chain")
        s_x = pair("x_loaded")
        s_a_var = sem("a_var_ready")
        s_a_pow = sem("a_rstd_ready")
        s_x0 = sem("x0_ready")
        s_a_tr = sem("x0_transposed")
        s_x0T = sem("x0T_in_sbuf")
        s_xt = sem("xt_tile_done")
        s_xt_out = sem("xt_tile_in_sbuf")
        s_table = pair("table_rows_stored")
        a_chain = sem("a_chain")
        s_index = sem("index_picked")
        s_gather = pair("rows_gathered")
        s_score = sem("scores_ready")
        s_exp = sem("scores_exp")
        s_x1 = sem("x1_ready")
        s_b_var = sem("b_var_ready")
        s_b_pow = sem("b_rstd_ready")
        s_x2 = sem("x2_ready")
        s_b_tr = sem("x2_transposed")
        s_x2T_hi = sem("x2T_hi_ready")
        s_x2T_lo = sem("x2T_lo_ready")
        s_acc0 = sem("residual_ready")
        s_logits = sem("logits_done")
        s_lshift = sem("logits_shifted")
        s_lexp = sem("logits_exp")
        s_comb = sem("combine_ready")
        s_comb_tr = sem("combine_transposed")
        s_combT = sem("combT_ready")
        b_chain = sem("b_chain")
        b2_chain = sem("b2_chain")
        s_h = sem("first_product_done")
        s_gelu = sem("gelu_done")
        s_hhi = sem("h_hi_ready")
        s_hlo = sem("h_lo_ready")
        s_y = sem("second_product_done")
        s_acc = sem("accumulated")
        s_out = pair("out_stored")

        def settle(eng):
            eng.sem_inc(s_settled, 1)

        def at_least(eng, s, count):
            if not isinstance(count, int) or count > 0:
                eng.wait_ge(s, count)

        class Chain:

            def __init__(self, eng, s, per_step):
                self.eng, self.s, self.per_step, self.base, self.k = eng, s, per_step, 0, 0

            def step(self, s):
                assert self.k in (0, self.per_step), self.k
                self.base, self.k = s * self.per_step, 0

            def __call__(self, ins):
                self.k += 1
                ins.then_inc(self.s, 1)
                self.eng.wait_ge(self.s, self.base + self.k)

        def shape(s):
            if isinstance(s, int) and s == FULL:
                return 1, TAIL_ROWS, TAIL_ROWS
            return GT, P, GROUP

        def tokens_of(ap, s):
            tiles, rows, n = shape(s)
            return ap[bass.ds(s * GROUP, n), :].rearrange("(t p) d -> p t d", p=rows)

        def x_of(s):
            tiles, rows, _ = shape(s)
            return x_all[0:rows, bass.ds(s * GT, tiles), :]

        def uses(c, j, b):
            halves = 1 if isinstance(c, int) and c == FULL else 2
            return c * USES + j * halves + b + 1

        def item_done(c, j):
            halves = 1 if isinstance(c, int) and c == FULL else 2
            return uses(c, j, halves - 1)

        def before(c, e, back):
            return (c, e - back) if e >= back else (c - 1, e - back + E)

        def exists(c):
            return not isinstance(c, int) or c >= 0

        def steps(eng, first, body):
            for s in range(first):
                body(s, s % 2)
            with eng.Fori(first // 2, FULL // 2) as i:
                for parity in range(2):
                    body(i * 2 + parity, parity, i)
            body(FULL, FULL % 2)

        def nth(s, parity, i):
            return s // 2 if i is None else i

        block = ctx.enter_context(nc.Block())

        @block.sync
        def _(sp):
            sp.dma_start(rows_in[:, 0, :][0:TILES - 1], dst[0:FULL * GROUP].rearrange("(t p) -> t p", p=P)).then_inc(s_small, 16)
            sp.dma_start(rows_in[TILES - 1:TILES, 0, 0:TAIL_ROWS], dst[FULL * GROUP:N].rearrange("(t p) -> t p", t=1)).then_inc(s_small, 16)
            sp.dma_start(rows_in[:, 1, :][0:TILES - 1], src[0:FULL * GROUP].rearrange("(t p) -> t p", p=P)).then_inc(s_small, 16)
            sp.dma_start(rows_in[TILES - 1:TILES, 1, 0:TAIL_ROWS], src[FULL * GROUP:N].rearrange("(t p) -> t p", t=1)).then_inc(s_small, 16)

            def a_step(s, parity, i=None):
                at_least(sp, s_x[parity], nth(s, parity, i) * 16)
                sp.dma_start(x_of(s), tokens_of(x, s)).then_inc(s_x[parity], 16)
                store(s - 3, 1 - parity)

            def store(s, parity):
                if isinstance(s, int) and s < 0:
                    return
                tiles, rows, _ = shape(s)
                sp.wait_ge(s_xt_out, s * GT + tiles)
                sp.dma_start(tokens_of(table, s), xt_out[0:rows, parity, 0:tiles, :]).then_inc(s_table[parity], 16)
                sp.dma_start(tokens_of(al_table, s), xt_out[0:rows, parity, 0:tiles, D + H:ROW]).then_inc(s_table[parity], 16)

            steps(sp, 4, a_step)
            for s in range(STEPS - 3, STEPS):
                store(s, s % 2)

            def c_step(s, parity, i=None):
                c = s - 2
                if exists(c):
                    put(c, parity)

            def put(c, parity):
                tiles, rows, _ = shape(c)
                sp.wait_ge(s_acc, item_done(c, E))
                sp.dma_start(tokens_of(out, c), acc[0:rows, parity, 0:tiles, :]).then_inc(s_out[parity], 16)

            steps(sp, 2, c_step)
            put(FULL - 1, (FULL - 1) % 2)
            put(FULL, FULL % 2)
            sp.wait_ge(s_out[0], 16 * ((STEPS + 1) // 2))
            sp.wait_ge(s_out[1], 16 * (STEPS // 2))

        @block.gpsimd
        def _(pool):
            nc.gpsimd.memset(ident[:], 1.0).then_inc(s_const, 1)
            pool.wait_ge(s_const, 1)
            nc.gpsimd.affine_select(out=ident[:], in_=ident[:], compare_op=ALU.is_equal, fill=0.0, base=0,
                                    pattern=[[-1, P]], channel_multiplier=1).then_inc(s_const, 1)
            pool.wait_ge(s_const, 2)
            nc.gpsimd.tensor_copy(ident16[:], ident[:]).then_inc(s_const, 1)
            nc.gpsimd.iota(iota8[:], pattern=[[1, E]], base=0, channel_multiplier=0,
                           allow_small_or_imprecise_dtypes=True).then_inc(s_const, 1)
            nc.gpsimd.memset(minus_half[:], -0.5).then_inc(s_const, 1)
            nc.gpsimd.memset(comb_parts[:], 0.0).then_inc(s_const, 1)
            pool.wait_ge(s_const, 6)

            def power(s, ready, done):
                tiles, rows, _ = shape(s)
                pool.wait_ge(ready, s + 1)
                nc.gpsimd.tensor_tensor(rstd_0[0:rows, 0:tiles], var_eps[0:rows, 0:tiles],
                                        minus_half[0:rows, 0:tiles], ALU.pow).then_inc(done, 1)

            steps(pool, 2, lambda s, parity, i=None: power(s, s_a_var, s_a_pow))

            pool.wait_ge(s_table[0], 32 * ((STEPS + 1) // 2))
            pool.wait_ge(s_table[1], 32 * (STEPS // 2))
            pool.wait_ge(s_setup, 1)

            def b_step(s, parity, i=None):
                tiles, rows, _ = shape(s)
                at_least(pool, s_x1, s - 1)
                nc.gpsimd.tensor_copy(index_now[0:rows, parity, :, 0:tiles],
                                      index[0:rows, :, bass.ds(s * GT, tiles)]).then_inc(s_index, 1)
                pool.wait_ge(s_index, s + 1)
                settle(pool)
                for t in range(tiles):
                    nc.gpsimd.indirect_dma_start(
                        out=xg[0:rows, parity, t, :], out_offset=None, in_=table,
                        in_offset=bass.IndirectOffsetOnAxis(ap=index_now[0:rows, parity, 0, t:t + 1], axis=0),
                    ).then_inc(s_gather[parity], 16)
                    nc.gpsimd.indirect_dma_start(
                        out=alg[0:rows, parity, t, :], out_offset=None, in_=al_table,
                        in_offset=bass.IndirectOffsetOnAxis(ap=index_now[0:rows, parity, 1, t:t + 1], axis=0),
                    ).then_inc(s_gather[parity], 16)
                power(s, s_b_var, s_b_pow)

            steps(pool, 2, b_step)

        @block.scalar
        def _(act):
            act.dma_start(wext[:, :, 0:D], weight.rearrange("(k p) n -> p k n", p=P)).then_inc(s_w, 16)
            for n, a in ((0, attn_r), (1, attn_l)):
                act.dma_start(attn[:, n, :, :], a.partition_broadcast(P)).then_inc(s_w, 16)
            act.dma_start(router_in[:], router_w).then_inc(s_small, 16)
            act.dma_start(b1_in[:], b1.rearrange("e (h f) -> (e h) f", h=HALVES)).then_inc(s_small, 16)
            for row in (0, 32, 64):
                act.dma_start(b2_in[row:row + E, :], b2).then_inc(s_small, 16)
            for n, w in ((0, w1), (1, w2)):
                act.dma_start(w_in[n][:], w.rearrange("e (k p) n -> p e k n", p=P)).then_inc(s_experts, 16)

            def a_step(s, parity, i=None):
                tiles, rows, n = shape(s)
                act.wait_ge(s_a_tr, s + 1)
                at_least(act, s_xt, (s - 1) * GT)
                for k in range(KT):
                    last = nc.scalar.copy(x0T[:, parity, k, 0:n], bank[4 + 2 * parity + k][:, 0:n])
                last.then_inc(s_x0T, 1)
                xt_rows(s - 1, 1 - parity, i if i is None else (i if parity else i - 1))

            def xt_rows(s, parity, stored):
                if not exists(s):
                    return
                tiles, rows, _ = shape(s)
                at_least(act, s_table[parity], 32 * (s // 2 if stored is None else stored))
                for t in range(tiles):
                    act.wait_ge(s_xt, s * GT + t + 1)
                    nc.scalar.copy(xt_out[0:rows, parity, t, :], bank[t][0:rows, 0:ROW]).then_inc(s_xt_out, 1)

            steps(act, 4, a_step)
            xt_rows(FULL, FULL % 2, None)

            def b_exp(s):
                tiles, rows, _ = shape(s)
                act.wait_ge(s_score, s + 1)
                nc.scalar.activation(expo[0:rows, 0:tiles, :], shifted[0:rows, 0:tiles, :], ACT.Exp).then_inc(s_exp, 1)

            def b_split(s, parity):
                _, _, n = shape(s)
                act.wait_ge(s_b_tr, s + 1)
                at_least(act, s_h, (s - 1) * E * HALVES)
                for k in range(KT):
                    last = nc.scalar.activation(x2T_hi[:, parity, k, 0:n], bank[6 + k][:, 0:n], ACT.Copy, scale=SPLIT)
                last.then_inc(s_x2T_hi, 1)

            def b_logit_exp(s):
                tiles, rows, _ = shape(s)
                act.wait_ge(s_lshift, s + 1)
                nc.scalar.activation(logit_exp[0:rows, 0:tiles, :], logit_shifted[0:rows, 0:tiles, :],
                                     ACT.Exp).then_inc(s_lexp, 1)

            def b_combT(s, parity):
                _, _, n = shape(s)
                act.wait_ge(s_comb_tr, s + 1)
                if exists(s - 1):
                    act.wait_ge(s_y, item_done(s - 1, 0))
                nc.scalar.copy(combT[:, parity, 0:n], bank[7][:].bitcast(fp16)[0:96, 0:n]).then_inc(s_combT, 1)

            def hidden(c, e):
                _, _, n = shape(c)
                q = c * E + e
                for f in range(HALVES):
                    act.wait_ge(s_h, q * HALVES + f + 1)
                    at_least(act, s_hlo, (q - 1) * HALVES)
                    nc.scalar.activation(h32[:, e % 2, f, 0:n], bank[2 * (e % 2) + f][:, 0:n], ACT.Gelu,
                                         bias=b1_col[:, e * HALVES + f:e * HALVES + f + 1],
                                         scale=UNSPLIT).then_inc(s_gelu, 1)
                pc, pe = before(c, e, RING_H)
                if exists(pc):
                    act.wait_ge(s_y, item_done(pc, 1 + pe))
                for f in range(HALVES):
                    act.wait_ge(s_gelu, q * HALVES + f + 1)
                    nc.scalar.activation(h_hi[:, e % RING_H, f, 0:n], h32[:, e % 2, f, 0:n], ACT.Copy,
                                         scale=SPLIT).then_inc(s_hhi, 1)

            def c_step(s, parity, i=None):
                c = s - 1
                for e in range(E):
                    if exists(c):
                        hidden(c, e)
                    if e == 0:
                        b_exp(s)
                    if e == 1 and exists(c):
                        b_combT(c, 1 - parity)
                    if e == 5:
                        b_split(s, parity)
                b_logit_exp(s)

            steps(act, 2, c_step)
            for e in range(E):
                hidden(FULL, e)
                if e == 1:
                    b_combT(FULL, FULL % 2)

        @block.vector
        def _(dve):
            link = Chain(dve, setup_chain, 0)
            dve.wait_ge(s_const, 6)
            dve.wait_ge(s_w, 48)
            for n in range(2):
                for k in range(KT):
                    link(nc.vector.tensor_tensor(attn_prod[:], wext[:, k, 0:D].rearrange("p (h c) -> p h c", h=H),
                                                 attn[:, n, :, :], ALU.mult))
                    ins = nc.vector.tensor_reduce(wext[:, k, D + n * H:D + (n + 1) * H], attn_prod[:], X, ALU.add)
                    link(ins)
            dve.sem_inc(s_wext, 1)
            dve.wait_ge(s_small, 16 * 9)
            nc.vector.memset(rows_f[:], 0.0)
            link(nc.vector.memset(b2_parts[:], 0.0))
            for n in range(2):
                nc.vector.tensor_copy(rows_f[0:TILES, n, 0:TAIL_ROWS], rows_in[0:TILES, n, 0:TAIL_ROWS])
                nc.vector.tensor_copy(rows_f[0:TILES - 1, n, TAIL_ROWS:P], rows_in[0:TILES - 1, n, TAIL_ROWS:P])
            link(nc.vector.memset(b2_hi[:], 0.0))
            dve.sem_inc(s_rows_f, 1)
            for row in (0, 32, 64):
                last = nc.vector.tensor_scalar(b2_hi[row:row + E, :], b2_in[row:row + E, :], SPLIT, None, ALU.mult)
            link(last)
            for row in (0, 64):
                nc.vector.tensor_copy(b2_parts[row:row + E, :], b2_hi[row:row + E, :])
            link(nc.vector.scalar_tensor_tensor(out=b2_parts[32:32 + E, :], in0=b2_in[32:32 + E, :], scalar=SPLIT,
                                                in1=b2_hi[32:32 + E, :], op0=ALU.mult, op1=ALU.subtract))
            dve.wait_ge(s_setup_tr, 1)
            nc.vector.tensor_scalar(router64[:], bank[0][:, 0:KT * E].rearrange("p (k e) -> p k e", k=KT), SPLIT, None, ALU.mult)
            nc.vector.tensor_copy(b1_col[:], bank[0][:, 16:16 + E * HALVES])
            link(nc.vector.tensor_copy(index[:], bank[0][:, 64:64 + 2 * TILES].rearrange("p (n t) -> p n t", n=2)))
            link(nc.vector.tensor_copy(router_hi[:], router64[:]))
            nc.vector.tensor_tensor(router_lo[:], router64[:], router_hi[:], ALU.subtract).then_inc(s_setup, 1)

            def norm_stats(link, rows, tiles, get):
                settle(dve)
                for t in range(tiles):
                    last = nc.vector.bn_stats(stats[0:rows, t, :], get(t))
                link(last)
                settle(dve)
                for t in range(tiles):
                    last = nc.vector.bn_aggr(mean_var[0:rows, t, :], stats[0:rows, t, :])
                link(last)
                return nc.vector.tensor_scalar(var_eps[0:rows, 0:tiles], mean_var[0:rows, 0:tiles, 1], EPS, None, ALU.add)

            def norm_rstd(link, rows, tiles):
                r, n = rstd_0[0:rows, 0:tiles], newton[0:rows, 0:tiles]
                link(nc.vector.tensor_tensor(n, r, r, ALU.mult))
                link(nc.vector.tensor_tensor(n, n, var_eps[0:rows, 0:tiles], ALU.mult))
                link(nc.vector.tensor_scalar(n, n, -0.5, 1.5, ALU.mult, ALU.add))
                link(nc.vector.tensor_tensor(rstd[0:rows, 0:tiles], r, n, ALU.mult))

            def normed(dst, src, rows, t):
                return nc.vector.tensor_scalar(dst, src, mean_var[0:rows, t, 0:1], rstd[0:rows, t:t + 1],
                                               ALU.subtract, ALU.mult)

            link_a = Chain(dve, a_chain, 6)

            def a_step(s, parity, i=None):
                tiles, rows, _ = shape(s)
                link_a.step(s)
                dve.wait_ge(s_x[parity], nth(s, parity, i) * 16 + 16)
                xs = x_of(s)
                norm_stats(link_a, rows, tiles, lambda t: xs[:, t, :]).then_inc(s_a_var, 1)
                dve.wait_ge(s_a_pow, s + 1)
                norm_rstd(link_a, rows, tiles)
                at_least(dve, s_a_tr, s - 1)
                for t in range(tiles):
                    last = normed(x0[0:rows, parity, t, :], xs[:, t, :], rows, t)
                last.then_inc(s_x0, 1)

            steps(dve, 2, a_step)

            dve.wait_ge(s_experts, 32)
            for n in range(2):
                flat = "p e k n -> p (e k n)"
                link(nc.vector.tensor_scalar(w_hi[n][:].rearrange(flat), w_in[n][:].rearrange(flat), SPLIT, None, ALU.mult))
                last = nc.vector.scalar_tensor_tensor(out=w_lo[n][:].rearrange(flat), in0=w_in[n][:].rearrange(flat),
                                                      scalar=SPLIT, in1=w_hi[n][:].rearrange(flat),
                                                      op0=ALU.mult, op1=ALU.subtract)
            last.then_inc(s_experts_split, 1)

            link_b = Chain(dve, b_chain, 16)
            link_b2 = Chain(dve, b2_chain, 14)

            def b_scores(s, parity, i):
                tiles, rows, _ = shape(s)
                link_b.step(s)
                sl = (slice(0, rows), slice(0, tiles))
                dve.wait_ge(s_gather[parity], nth(s, parity, i) * (32 * GT) + 32 * tiles)
                link_b(nc.vector.tensor_tensor(score[sl], xg[0:rows, parity, 0:tiles, D:D + H],
                                               alg[0:rows, parity, 0:tiles, :], ALU.add))
                link_b(nc.vector.scalar_tensor_tensor(out=lrelu[sl], in0=score[sl], scalar=SLOPE, in1=score[sl],
                                                      op0=ALU.mult, op1=ALU.max))
                link_b(nc.vector.tensor_reduce(top[sl], lrelu[sl], X, ALU.max))
                nc.vector.tensor_tensor(shifted[sl], lrelu[sl], top[sl].unsqueeze(2).to_broadcast([rows, tiles, H]),
                                        ALU.subtract).then_inc(s_score, 1)

            def b_message(s, parity):
                tiles, rows, _ = shape(s)
                sl = (slice(0, rows), slice(0, tiles))
                dve.wait_ge(s_exp, s + 1)
                link_b(nc.vector.tensor_reduce(total[sl], expo[sl], X, ALU.add))
                link_b(nc.vector.reciprocal(inverse[sl], total[sl]))
                link_b(nc.vector.tensor_tensor(alpha[sl], expo[sl], inverse[sl].unsqueeze(2).to_broadcast([rows, tiles, H]), ALU.mult))
                link_b(nc.vector.tensor_tensor(prod[sl], xg[0:rows, parity, 0:tiles, 0:D].rearrange("p t (h c) -> p t h c", h=H),
                                               alpha[sl].unsqueeze(3).to_broadcast([rows, tiles, H, C]), ALU.mult))
                link_b(nc.vector.tensor_reduce(tmp[sl], prod[sl].rearrange("p t h c -> p t c h"), X, ALU.add))

            def b_residual(s):
                tiles, rows, _ = shape(s)
                sl = (slice(0, rows), slice(0, tiles))
                xs = x_of(s)
                xh = xs.rearrange("p t (h c) -> p t h c", h=H)
                ins = nc.vector.tensor_tensor(xh, xh, tmp[sl].unsqueeze(2).to_broadcast([rows, tiles, H, C]), ALU.add)
                ins.then_inc(s_x1, 1)
                dve.wait_ge(s_x1, s + 1)
                norm_stats(link_b, rows, tiles, lambda t: xs[:, t, :]).then_inc(s_b_var, 1)

            def b_norm(s):
                tiles, rows, _ = shape(s)
                xs = x_of(s)
                dve.wait_ge(s_b_pow, s + 1)
                norm_rstd(link_b, rows, tiles)
                at_least(dve, s_b_tr, s)
                for t in range(tiles):
                    last = normed(x2[0:rows, t, :], xs[:, t, :], rows, t)
                last.then_inc(s_x2, 1)

            def b_split(s, parity, i):
                tiles, rows, n = shape(s)
                dve.wait_ge(s_x2T_hi, s + 1)
                for k in range(KT):
                    last = nc.vector.scalar_tensor_tensor(out=x2T_lo[:, parity, k, 0:n], in0=bank[6 + k][:, 0:n], scalar=SPLIT,
                                                          in1=x2T_hi[:, parity, k, 0:n], op0=ALU.mult, op1=ALU.subtract)
                last.then_inc(s_x2T_lo, 1)
                dve.wait_ge(s_x2, s + 1)
                at_least(dve, s_out[parity], nth(s, parity, i) * 16)
                nc.vector.tensor_tensor(acc[0:rows, parity, 0:tiles, :], x_of(s), x2[0:rows, 0:tiles, :],
                                        ALU.add).then_inc(s_acc0, 1)

            def b_logits(s):
                tiles, rows, _ = shape(s)
                sl = (slice(0, rows), slice(0, tiles))
                dve.wait_ge(s_logits, s + 1)
                link_b(nc.vector.tensor_scalar(logits[sl], bank[6][0:rows, 0:tiles * E].rearrange("p (t e) -> p t e", e=E),
                                               UNSPLIT, None, ALU.mult))
                link_b(nc.vector.tensor_reduce(logit_top[sl], logits[sl], X, ALU.max))
                nc.vector.tensor_tensor(logit_shifted[sl], logits[sl], logit_top[sl].unsqueeze(2).to_broadcast([rows, tiles, E]),
                                        ALU.subtract).then_inc(s_lshift, 1)

            def b_route(s, parity):
                tiles, rows, _ = shape(s)
                sl = (slice(0, rows), slice(0, tiles))
                link_b2.step(s)
                wide = [rows, tiles, E]
                dve.wait_ge(s_lexp, s + 1)
                link_b2(nc.vector.tensor_reduce(prob_total[sl], logit_exp[sl], X, ALU.add))
                link_b2(nc.vector.reciprocal(prob_inverse[sl], prob_total[sl]))
                link_b2(nc.vector.tensor_tensor(prob[sl], logit_exp[sl], prob_inverse[sl].unsqueeze(2).to_broadcast(wide), ALU.mult))
                settle(dve)
                for t in range(tiles):
                    last = nc.vector.max(best[0:rows, t, :], prob[0:rows, t, :])
                link_b2(last)
                settle(dve)
                for t in range(tiles):
                    last = nc.vector.max_index(best_index[0:rows, t, :], best[0:rows, t, :], prob[0:rows, t, :])
                link_b2(last)
                link_b2(nc.vector.tensor_copy(best_f[sl], best_index[0:rows, 0:tiles, 0:TOP_K]))
                for n in range(TOP_K):
                    last = nc.vector.tensor_tensor(mask[0:rows, n, 0:tiles, :], iota8[0:rows].unsqueeze(1).to_broadcast(wide),
                                                   best_f[0:rows, 0:tiles, n:n + 1].to_broadcast(wide), ALU.is_equal)
                link_b2(last)
                link_b2(nc.vector.tensor_tensor(mask[0:rows, 0, 0:tiles, :], mask[0:rows, 0, 0:tiles, :],
                                                mask[0:rows, 1, 0:tiles, :], ALU.add))
                link_b2(nc.vector.tensor_tensor(kept[sl], mask[0:rows, 0, 0:tiles, :], prob[sl], ALU.mult))
                link_b2(nc.vector.tensor_reduce(prob_total[sl], kept[sl], X, ALU.add))
                link_b2(nc.vector.tensor_scalar(prob_total[sl], prob_total[sl], 1e-12, None, ALU.max))
                link_b2(nc.vector.reciprocal(prob_inverse[sl], prob_total[sl]))
                link_b2(nc.vector.scalar_tensor_tensor(out=comb64[sl], in0=kept[sl], scalar=SPLIT,
                                                       in1=prob_inverse[sl].unsqueeze(2).to_broadcast(wide),
                                                       op0=ALU.mult, op1=ALU.mult))
                at_least(dve, s_comb_tr, s)
                nc.vector.tensor_copy(comb_parts[0:rows, 0:tiles, 0:E], comb64[sl])
                nc.vector.tensor_copy(comb_parts[0:rows, 0:tiles, 32:32 + E], comb64[sl])
                link_b2(nc.vector.tensor_scalar(comb[0:rows, parity, 0:tiles, :], comb64[sl], UNSPLIT / SPLIT, None, ALU.mult))
                nc.vector.tensor_tensor(comb_parts[0:rows, 0:tiles, 64:64 + E], comb64[sl], comb_parts[0:rows, 0:tiles, 0:E],
                                        ALU.subtract).then_inc(s_comb, 1)

            def remainder(c, e):
                _, _, n = shape(c)
                q = c * E + e
                for f in range(HALVES):
                    dve.wait_ge(s_hhi, q * HALVES + f + 1)
                    nc.vector.scalar_tensor_tensor(out=h_lo[:, e % RING_H, f, 0:n], in0=h32[:, e % 2, f, 0:n], scalar=SPLIT,
                                                   in1=h_hi[:, e % RING_H, f, 0:n], op0=ALU.mult,
                                                   op1=ALU.subtract).then_inc(s_hlo, 1)

            def accumulate(c, j, parity):
                tiles, rows, _ = shape(c)
                if j == 0:
                    dve.wait_ge(s_acc0, c + 1)
                for b in range(-(-tiles // 2)):
                    u = uses(c, j, b)
                    dve.wait_ge(s_y, u)
                    at_least(dve, s_acc, u - (2 if tiles > 1 else 1))
                    y = bank[4 + (b if tiles > 1 else j % 2)]
                    for t in range(2 * b, min(tiles, 2 * b + 2)):
                        a = acc[0:rows, parity, t, :]
                        weight_of = UNSPLIT if j == 0 else comb[0:rows, parity, t, j - 1:j]
                        last = nc.vector.scalar_tensor_tensor(out=a, in0=y[0:rows, (t % 2) * D:(t % 2 + 1) * D], scalar=weight_of,
                                                              in1=a, op0=ALU.mult, op1=ALU.add)
                    last.then_inc(s_acc, 1)

            def finish(c, e, parity):
                pc, pe = before(c, e, LAG)
                if pe == 0:
                    accumulate(pc, 0, parity)
                if exists(pc):
                    accumulate(pc, 1 + pe, parity if e >= LAG else 1 - parity)

            def c_step(s, parity, i=None):
                c = s - 1
                for e in range(E):
                    if exists(c):
                        remainder(c, e)
                        if e == 0:
                            b_route(c, 1 - parity)
                        finish(c, e, 1 - parity)
                    if e == 0:
                        b_scores(s, parity, i)
                    if e == 1:
                        b_message(s, parity)
                    if e == 2:
                        b_residual(s)
                    if e == 3:
                        b_norm(s)
                    if e == 6:
                        b_split(s, parity, i)
                b_logits(s)

            steps(dve, 2, c_step)
            for e in range(E):
                remainder(FULL, e)
                if e == 0:
                    b_route(FULL, FULL % 2)
                finish(FULL, e, FULL % 2)
            for e in range(E - LAG, E):
                accumulate(FULL, 1 + e, FULL % 2)

        @block.tensor
        def _(pe):
            pe.wait_ge(s_const, 6)
            pe.wait_ge(s_small, 16 * 9)
            pe.wait_ge(s_rows_f, 1)
            for k in range(KT):
                nc.tensor.transpose(bank[0][:, k * E:(k + 1) * E], router_in[:, k * P:(k + 1) * P], ident[0:E, 0:E])
            nc.tensor.transpose(bank[0][:, 16:16 + E * HALVES], b1_in[:], ident[0:E * HALVES, 0:E * HALVES])
            for n in range(2):
                last = nc.tensor.transpose(bank[0][:, 64 + n * TILES:64 + (n + 1) * TILES], rows_f[:, n, :],
                                           ident[0:TILES, 0:TILES])
            last.then_inc(s_setup_tr, 1)
            pe.wait_ge(s_setup, 1)
            pe.wait_ge(s_wext, 1)

            def a_step(s, parity, i=None):
                tiles, rows, _ = shape(s)
                pe.wait_ge(s_x0, s + 1)
                at_least(pe, s_x0T, s - 1)
                for k in range(KT):
                    for t in range(tiles):
                        last = nc.tensor.transpose(bank[4 + 2 * parity + k][:, t * P:t * P + rows],
                                                   x0[0:rows, parity, t, k * P:(k + 1) * P], ident[0:rows, 0:rows])
                last.then_inc(s_a_tr, 1)
                xt_product(s - 1, 1 - parity)

            def xt_product(s, parity):
                if not exists(s):
                    return
                tiles, rows, _ = shape(s)
                pe.wait_ge(s_x0T, s + 1)
                for t in range(tiles):
                    at_least(pe, s_xt_out, (s - 1) * GT + t + 1)
                    for k in range(KT):
                        last = nc.tensor.matmul(bank[t][0:rows, 0:ROW], x0T[:, parity, k, t * P:t * P + rows], wext[:, k, :],
                                                start=(k == 0), stop=(k == KT - 1))
                    last.then_inc(s_xt, 1)

            steps(pe, 4, a_step)
            xt_product(FULL, FULL % 2)

            def b_transpose(s):
                tiles, rows, _ = shape(s)
                pe.wait_ge(s_x2, s + 1)
                at_least(pe, s_lshift, s)
                at_least(pe, s_combT, s)
                for k in range(KT):
                    for t in range(tiles):
                        last = nc.tensor.transpose(bank[6 + k][:, t * P:t * P + rows], x2[0:rows, t, k * P:(k + 1) * P],
                                                   ident[0:rows, 0:rows])
                last.then_inc(s_b_tr, 1)

            def b_router(s, parity):
                tiles, rows, _ = shape(s)
                pe.wait_ge(s_x2T_lo, s + 1)
                for t in range(tiles):
                    parts = [(x, w, k) for k in range(KT)
                             for x, w in ((x2T_hi, router_hi), (x2T_hi, router_lo), (x2T_lo, router_hi))]
                    for n, (xp, wp, k) in enumerate(parts):
                        last = nc.tensor.matmul(bank[6][0:rows, t * E:(t + 1) * E], xp[:, parity, k, t * P:t * P + rows], wp[:, k, :],
                                                start=(n == 0), stop=(n == len(parts) - 1))
                last.then_inc(s_logits, 1)

            def b_combine(s):
                tiles, rows, _ = shape(s)
                pe.wait_ge(s_comb, s + 1)
                for t in range(tiles):
                    last = nc.tensor.transpose(bank[7][:].bitcast(fp16)[0:96, t * P:t * P + rows], comb_parts[0:rows, t, :],
                                               ident16[0:rows, 0:rows])
                last.then_inc(s_comb_tr, 1)

            def first(c, e, parity):
                _, _, n = shape(c)
                q = c * E + e
                for f in range(HALVES):
                    at_least(pe, s_gelu, (q - 2) * HALVES + f + 1)
                    parts = [(w, x, k) for k in range(KT)
                             for w, x in ((w_hi[0], x2T_hi), (w_hi[0], x2T_lo), (w_lo[0], x2T_hi))]
                    for m, (wp, xp, k) in enumerate(parts):
                        last = nc.tensor.matmul(bank[2 * (e % 2) + f][:, 0:n], wp[:, e, k, f * P:(f + 1) * P],
                                                xp[:, parity, k, 0:n], start=(m == 0), stop=(m == len(parts) - 1))
                    last.then_inc(s_h, 1)

            def bias(c, parity):
                pe.wait_ge(s_combT, c + 1)
                output(c, 0, lambda t, rows: [(combT[:, parity, t * P:t * P + rows], b2_parts[:])])

            def second(c, e):
                pe.wait_ge(s_hlo, (c * E + e + 1) * HALVES)
                r = e % RING_H
                output(c, 1 + e, lambda t, rows: [
                    (hp[:, r, f, t * P:t * P + rows], wp[:, e, f, :]) for f in range(HALVES)
                    for hp, wp in ((h_hi, w_hi[1]), (h_hi, w_lo[1]), (h_lo, w_hi[1]))])

            def output(c, j, parts_of):
                tiles, rows, _ = shape(c)
                for b in range(-(-tiles // 2)):
                    u = uses(c, j, b)
                    at_least(pe, s_acc, u - 2)
                    y = bank[4 + (b if tiles > 1 else j % 2)]
                    for t in range(2 * b, min(tiles, 2 * b + 2)):
                        parts = parts_of(t, rows)
                        for m, (lhsT, rhs) in enumerate(parts):
                            last = nc.tensor.matmul(y[0:rows, (t % 2) * D:(t % 2 + 1) * D], lhsT, rhs,
                                                    start=(m == 0), stop=(m == len(parts) - 1))
                    last.then_inc(s_y, 1)

            def seconds(c, e, parity):
                pc, pe_ = before(c, e, LAG)
                if pe_ == 0:
                    bias(pc, parity)
                if exists(pc):
                    second(pc, pe_)

            pe.wait_ge(s_experts_split, 1)

            def c_step(s, parity, i=None):
                c = s - 1
                for e in range(E):
                    if exists(c):
                        first(c, e, 1 - parity)
                    if e == 5:
                        b_transpose(s)
                    if e == 7:
                        b_router(s, parity)
                    if e == 1 and exists(c):
                        b_combine(c)
                    if exists(c):
                        seconds(c, e, 1 - parity)

            steps(pe, 2, c_step)
            for e in range(E):
                first(FULL, e, FULL % 2)
                if e == 1:
                    b_combine(FULL)
                seconds(FULL, e, FULL % 2)
            for e in range(E - LAG, E):
                second(FULL, e)


_INS = ['x', 'src', 'dst', 'L0_gnn_weight', 'L0_gnn_attn_l', 'L0_gnn_attn_r', 'L0_ffn_router_w', 'L0_ffn_w1',
        'L0_ffn_b1', 'L0_ffn_w2', 'L0_ffn_b2']
_OUTS = [((N, D), 'float32')]


def kernel(**inputs):
    import numpy as _np
    import concourse.bacc as _bacc
    from concourse import mybir as _mybir
    from concourse.bass_utils import run_bass_kernel_spmd as _run

    nc = _bacc.Bacc("TRN2", target_bir_lowering=False, num_devices=1)
    arrays, args = {}, []
    for name in _INS:
        a = _np.ascontiguousarray(inputs[name])
        arrays[f"in_{name}_dram"] = a
        args.append(nc.dram_tensor(f"in_{name}_dram", a.shape, _mybir.dt.from_np(a.dtype), kind="ExternalInput").ap())
    for i, (shape, dtype) in enumerate(_OUTS):
        dt = _mybir.dt.from_np(_np.dtype(dtype))
        args.append(nc.dram_tensor(f"out_{i}_dram", shape, dt, kind="ExternalOutput").ap())
    build(nc, *args)
    r = _run(nc, [arrays], core_ids=[0])
    got = tuple(r.results[0][f"out_{i}_dram"] for i in range(len(_OUTS)))
    return got[0]
```

```python
import concourse.bass as bass
from concourse import mybir
from contextlib import ExitStack

N, D, H, C, E, TOP_K = 6250, 256, 4, 64, 8, 2
P = 128
KT = D // P
GT = 4
GROUP = GT * P
FULL = N // GROUP
TILES = -(-N // P)
TAIL_ROWS = N - FULL * GROUP
STEPS = FULL + 1
ROW = D + 2 * H
EPS = 1e-5
SLOPE = 0.01
SPLIT = 64.0
UNSPLIT = 1.0 / (SPLIT * SPLIT)
HALVES = 2
USES = 2 * (E + 1)
RING_H = 4
H_WORDS = RING_H * HALVES * GROUP
LAG = 2

assert TAIL_ROWS <= P and TILES == FULL * GT + 1 and FULL % 2 == 0


def build(nc, x, src, dst, weight, attn_l, attn_r, router_w, w1, b1, w2, b2, out):
    fp32, fp16 = mybir.dt.float32, mybir.dt.float16
    i32, u32 = mybir.dt.int32, mybir.dt.uint32
    ALU = mybir.AluOpType
    ACT = mybir.ActivationFunctionType
    X = mybir.AxisListType.X

    table = nc.dram_tensor("xt_table", (N, ROW), fp32, kind="Internal").ap()
    al_table = nc.dram_tensor("al_table", (N, H), fp32, kind="Internal").ap()

    ctx = ExitStack()
    with ctx:
        def sb(name, shape, dt=fp32):
            return ctx.enter_context(nc.sbuf_tensor(name, shape, dt))

        def sem(name):
            return ctx.enter_context(nc.semaphore(name))

        def pair(name):
            return [sem(f"{name}{i}") for i in range(2)]

        bank = [ctx.enter_context(nc.psum_tensor(f"bank{i}", [P, 512], fp32)) for i in range(8)]

        ident = sb("ident", [P, P])
        ident16 = sb("ident16", [P, P], fp16)
        iota8 = sb("iota8", [P, E])
        minus_half = sb("minus_half", [P, GT])
        wext = sb("wext", [P, KT, ROW])
        attn = sb("attn", [P, 2, H, C])
        attn_prod = sb("attn_prod", [P, H, C])
        rows_in = sb("rows_in", [TILES, 2, P], i32)
        rows_f = sb("rows_f", [TILES, 2, P])
        index = sb("index", [P, 2, TILES], u32)
        index_now = sb("index_now", [P, 2, 2, GT], u32)
        router_in = sb("router_in", [E, D])
        router64 = sb("router64", [P, KT, E])
        router_hi = sb("router_hi", [P, KT, E], fp16)
        router_lo = sb("router_lo", [P, KT, E], fp16)
        b1_in = sb("b1_in", [E * HALVES, P])
        b1_col = sb("b1_col", [P, E * HALVES])
        b2_in = sb("b2_in", [96, D])
        b2_hi = sb("b2_hi", [96, D], fp16)
        b2_parts = sb("b2_parts", [96, D], fp16)
        w_in = [sb(f"w{n}_in", [P, E, KT, D]) for n in (1, 2)]
        w_hi = [sb(f"w{n}_hi", [P, E, KT, D], fp16) for n in (1, 2)]
        w_lo = [sb(f"w{n}_lo", [P, E, KT, D], fp16) for n in (1, 2)]
        x_all = sb("x_all", [P, TILES, D])
        stats = sb("stats", [P, GT, 6])
        mean_var = sb("mean_var", [P, GT, 2])
        var_eps = sb("var_eps", [P, GT])
        rstd_0 = sb("rstd_0", [P, GT])
        newton = sb("newton", [P, GT])
        rstd = sb("rstd", [P, GT])
        x0 = sb("x0", [P, 2, GT, D])
        x0T = sb("x0T", [P, 2, KT, GROUP])
        xt_out = sb("xt_out", [P, 2, GT, ROW])
        xg = sb("xg", [P, 2, GT, ROW])
        alg = sb("alg", [P, 2, GT, H])
        score = sb("score", [P, GT, H])
        lrelu = sb("lrelu", [P, GT, H])
        top = sb("top", [P, GT])
        shifted = sb("shifted", [P, GT, H])
        expo = sb("expo", [P, GT, H])
        total = sb("total", [P, GT])
        inverse = sb("inverse", [P, GT])
        alpha = sb("alpha", [P, GT, H])
        prod = sb("prod", [P, GT, H, C])
        tmp = sb("tmp", [P, GT, C])
        x2 = sb("x2", [P, GT, D])
        x2T_hi = sb("x2T_hi", [P, 2, KT, GROUP], fp16)
        x2T_lo = sb("x2T_lo", [P, 2, KT, GROUP], fp16)
        logits = sb("logits", [P, GT, E])
        logit_top = sb("logit_top", [P, GT])
        logit_shifted = sb("logit_shifted", [P, GT, E])
        logit_exp = sb("logit_exp", [P, GT, E])
        prob_total = sb("prob_total", [P, GT])
        prob_inverse = sb("prob_inverse", [P, GT])
        prob = sb("prob", [P, GT, E])
        best = sb("best", [P, GT, 8])
        best_index = sb("best_index", [P, GT, 8], u32)
        best_f = sb("best_f", [P, GT, TOP_K])
        mask = sb("mask", [P, 2, GT, E])
        kept = sb("kept", [P, GT, E])
        comb = sb("comb", [P, 2, GT, E])
        comb64 = sb("comb64", [P, GT, E])
        comb_parts = sb("comb_parts", [P, GT, 96], fp16)
        combT = sb("combT", [96, 2, GROUP], fp16)
        acc = sb("acc", [P, 2, GT, D])
        h32 = sb("h32", [P, 2, HALVES, GROUP])
        h_hi, h_lo = [w_in[0][:].rearrange("p e k n -> p (e k n)").bitcast(fp16)[:, n * H_WORDS:(n + 1) * H_WORDS].rearrange(
            "p (r f n) -> p r f n", r=RING_H, f=HALVES) for n in range(2)]

        s_settled = sem("waits_settled")
        s_w = sem("gnn_weights_loaded")
        s_small = sem("small_inputs_loaded")
        s_experts = sem("expert_weights_loaded")
        s_const = sem("constants_made")
        s_rows_f = sem("edge_rows_as_float")
        s_setup_tr = sem("setup_transposed")
        s_setup = sem("setup_evacuated")
        s_wext = sem("wext_made")
        s_experts_split = sem("expert_weights_split")
        setup_chain = sem("setup_chain")
        s_x = pair("x_loaded")
        s_a_var = sem("a_var_ready")
        s_a_pow = sem("a_rstd_ready")
        s_x0 = sem("x0_ready")
        s_a_tr = sem("x0_transposed")
        s_x0T = sem("x0T_in_sbuf")
        s_xt = sem("xt_tile_done")
        s_xt_out = sem("xt_tile_in_sbuf")
        s_table = pair("table_rows_stored")
        a_chain = sem("a_chain")
        s_index = sem("index_picked")
        s_gather = pair("rows_gathered")
        s_score = sem("scores_ready")
        s_exp = sem("scores_exp")
        s_alpha = sem("alpha_ready")
        s_prod = sem("rows_weighted")
        s_tmp = sem("message_ready")
        s_x1 = sem("x1_ready")
        s_b_var = sem("b_var_ready")
        s_b_pow = sem("b_rstd_ready")
        s_x2 = sem("x2_ready")
        s_b_tr = sem("x2_transposed")
        s_x2T_hi = sem("x2T_hi_ready")
        s_x2T_lo = sem("x2T_lo_ready")
        s_acc0 = sem("residual_ready")
        s_logits = sem("logits_done")
        s_lshift = sem("logits_shifted")
        s_lexp = sem("logits_exp")
        s_comb = sem("combine_ready")
        s_comb_tr = sem("combine_transposed")
        s_combT = sem("combT_ready")
        b_chain = sem("b_chain")
        b2_chain = sem("b2_chain")
        s_h = sem("first_product_done")
        s_gelu = sem("gelu_done")
        s_hhi = sem("h_hi_ready")
        s_hlo = sem("h_lo_ready")
        s_y = sem("second_product_done")
        s_acc = sem("accumulated")
        s_out = pair("out_stored")

        def settle(eng):
            eng.sem_inc(s_settled, 1)

        def at_least(eng, s, count):
            if not isinstance(count, int) or count > 0:
                eng.wait_ge(s, count)

        class Chain:

            def __init__(self, eng, s, per_step):
                self.eng, self.s, self.per_step, self.base, self.k = eng, s, per_step, 0, 0

            def step(self, s):
                assert self.k in (0, self.per_step), self.k
                self.base, self.k = s * self.per_step, 0

            def __call__(self, ins):
                self.k += 1
                ins.then_inc(self.s, 1)
                self.eng.wait_ge(self.s, self.base + self.k)

        def shape(s):
            if isinstance(s, int) and s == FULL:
                return 1, TAIL_ROWS, TAIL_ROWS
            return GT, P, GROUP

        def tokens_of(ap, s):
            tiles, rows, n = shape(s)
            return ap[bass.ds(s * GROUP, n), :].rearrange("(t p) d -> p t d", p=rows)

        def x_of(s):
            tiles, rows, _ = shape(s)
            return x_all[0:rows, bass.ds(s * GT, tiles), :]

        def uses(c, j, b):
            halves = 1 if isinstance(c, int) and c == FULL else 2
            return c * USES + j * halves + b + 1

        def item_done(c, j):
            halves = 1 if isinstance(c, int) and c == FULL else 2
            return uses(c, j, halves - 1)

        def before(c, e, back):
            return (c, e - back) if e >= back else (c - 1, e - back + E)

        def exists(c):
            return not isinstance(c, int) or 0 <= c <= FULL

        def steps(eng, first, body, extra=0):
            for s in range(first):
                body(s, s % 2)
            with eng.Fori(first // 2, FULL // 2) as i:
                for parity in range(2):
                    body(i * 2 + parity, parity, i)
            for s in range(FULL, FULL + 1 + extra):
                body(s, s % 2)

        def nth(s, parity, i):
            return s // 2 if i is None else i

        block = ctx.enter_context(nc.Block())

        @block.sync
        def _(sp):
            sp.dma_start(rows_in[:, 0, :][0:TILES - 1], dst[0:FULL * GROUP].rearrange("(t p) -> t p", p=P)).then_inc(s_small, 16)
            sp.dma_start(rows_in[TILES - 1:TILES, 0, 0:TAIL_ROWS], dst[FULL * GROUP:N].rearrange("(t p) -> t p", t=1)).then_inc(s_small, 16)
            sp.dma_start(rows_in[:, 1, :][0:TILES - 1], src[0:FULL * GROUP].rearrange("(t p) -> t p", p=P)).then_inc(s_small, 16)
            sp.dma_start(rows_in[TILES - 1:TILES, 1, 0:TAIL_ROWS], src[FULL * GROUP:N].rearrange("(t p) -> t p", t=1)).then_inc(s_small, 16)

            def a_step(s, parity, i=None):
                at_least(sp, s_x[parity], nth(s, parity, i) * 16)
                sp.dma_start(x_of(s), tokens_of(x, s)).then_inc(s_x[parity], 16)
                store(s - 3, 1 - parity)

            def store(s, parity):
                if isinstance(s, int) and s < 0:
                    return
                tiles, rows, _ = shape(s)
                sp.wait_ge(s_xt_out, s * GT + tiles)
                sp.dma_start(tokens_of(table, s), xt_out[0:rows, parity, 0:tiles, :]).then_inc(s_table[parity], 16)
                sp.dma_start(tokens_of(al_table, s), xt_out[0:rows, parity, 0:tiles, D + H:ROW]).then_inc(s_table[parity], 16)

            steps(sp, 4, a_step)
            for s in range(STEPS - 3, STEPS):
                store(s, s % 2)

            def c_step(s, parity, i=None):
                c = s - 2
                if exists(c):
                    put(c, parity)

            def put(c, parity):
                tiles, rows, _ = shape(c)
                sp.wait_ge(s_acc, item_done(c, E))
                sp.dma_start(tokens_of(out, c), acc[0:rows, parity, 0:tiles, :]).then_inc(s_out[parity], 16)

            steps(sp, 2, c_step, 2)
            sp.wait_ge(s_out[0], 16 * ((STEPS + 1) // 2))
            sp.wait_ge(s_out[1], 16 * (STEPS // 2))

        @block.gpsimd
        def _(pool):
            nc.gpsimd.memset(ident[:], 1.0).then_inc(s_const, 1)
            pool.wait_ge(s_const, 1)
            nc.gpsimd.affine_select(out=ident[:], in_=ident[:], compare_op=ALU.is_equal, fill=0.0, base=0,
                                    pattern=[[-1, P]], channel_multiplier=1).then_inc(s_const, 1)
            pool.wait_ge(s_const, 2)
            nc.gpsimd.tensor_copy(ident16[:], ident[:]).then_inc(s_const, 1)
            nc.gpsimd.iota(iota8[:], pattern=[[1, E]], base=0, channel_multiplier=0,
                           allow_small_or_imprecise_dtypes=True).then_inc(s_const, 1)
            nc.gpsimd.memset(minus_half[:], -0.5).then_inc(s_const, 1)
            nc.gpsimd.memset(comb_parts[:], 0.0).then_inc(s_const, 1)
            pool.wait_ge(s_const, 6)

            def power(s, ready, done):
                tiles, rows, _ = shape(s)
                pool.wait_ge(ready, s + 1)
                nc.gpsimd.tensor_tensor(rstd_0[0:rows, 0:tiles], var_eps[0:rows, 0:tiles],
                                        minus_half[0:rows, 0:tiles], ALU.pow).then_inc(done, 1)

            steps(pool, 2, lambda s, parity, i=None: power(s, s_a_var, s_a_pow))

            pool.wait_ge(s_table[0], 32 * ((STEPS + 1) // 2))
            pool.wait_ge(s_table[1], 32 * (STEPS // 2))
            pool.wait_ge(s_setup, 1)

            def gather(s, parity):
                tiles, rows, _ = shape(s)
                at_least(pool, s_prod, s - 1)
                nc.gpsimd.tensor_copy(index_now[0:rows, parity, :, 0:tiles],
                                      index[0:rows, :, bass.ds(s * GT, tiles)]).then_inc(s_index, 1)
                pool.wait_ge(s_index, s + 1)
                settle(pool)
                for t in range(tiles):
                    nc.gpsimd.indirect_dma_start(
                        out=xg[0:rows, parity, t, :], out_offset=None, in_=table,
                        in_offset=bass.IndirectOffsetOnAxis(ap=index_now[0:rows, parity, 0, t:t + 1], axis=0),
                    ).then_inc(s_gather[parity], 16)
                    nc.gpsimd.indirect_dma_start(
                        out=alg[0:rows, parity, t, :], out_offset=None, in_=al_table,
                        in_offset=bass.IndirectOffsetOnAxis(ap=index_now[0:rows, parity, 1, t:t + 1], axis=0),
                    ).then_inc(s_gather[parity], 16)

            def b_step(s, parity, i=None):
                if exists(s):
                    gather(s, parity)
                if exists(s - 1):
                    message(s - 1, 1 - parity)
                    power(s - 1, s_b_var, s_b_pow)
                    residual(s - 1, 1 - parity, (s - 1) // 2 if i is None else (i if parity else i - 1))

            def message(s, parity):
                tiles, rows, _ = shape(s)
                sl = (slice(0, rows), slice(0, tiles))
                pool.wait_ge(s_alpha, s + 1)
                nc.gpsimd.tensor_tensor(prod[sl], xg[0:rows, parity, 0:tiles, 0:D].rearrange("p t (h c) -> p t h c", h=H),
                                        alpha[sl].unsqueeze(3).to_broadcast([rows, tiles, H, C]), ALU.mult).then_inc(s_prod, 1)
                pool.wait_ge(s_tmp, s + 1)
                xh = x_of(s).rearrange("p t (h c) -> p t h c", h=H)
                settle(pool)
                nc.gpsimd.tensor_tensor(xh, xh, tmp[sl].unsqueeze(2).to_broadcast([rows, tiles, H, C]),
                                        ALU.add).then_inc(s_x1, 1)

            def residual(s, parity, before_it):
                tiles, rows, _ = shape(s)
                pool.wait_ge(s_x2, s + 1)
                pool.wait_ge(s_x1, s + 1)
                if exists(s - 2):
                    pool.wait_ge(s_out[parity], 16 * before_it)
                settle(pool)
                nc.gpsimd.tensor_tensor(acc[0:rows, parity, 0:tiles, :], x_of(s), x2[0:rows, 0:tiles, :],
                                        ALU.add).then_inc(s_acc0, 1)

            steps(pool, 4, b_step, 1)

        @block.scalar
        def _(act):
            act.dma_start(wext[:, :, 0:D], weight.rearrange("(k p) n -> p k n", p=P)).then_inc(s_w, 16)
            for n, a in ((0, attn_r), (1, attn_l)):
                act.dma_start(attn[:, n, :, :], a.partition_broadcast(P)).then_inc(s_w, 16)
            act.dma_start(router_in[:], router_w).then_inc(s_small, 16)
            act.dma_start(b1_in[:], b1.rearrange("e (h f) -> (e h) f", h=HALVES)).then_inc(s_small, 16)
            for row in (0, 32, 64):
                act.dma_start(b2_in[row:row + E, :], b2).then_inc(s_small, 16)
            for n, w in ((0, w1), (1, w2)):
                act.dma_start(w_in[n][:], w.rearrange("e (k p) n -> p e k n", p=P)).then_inc(s_experts, 16)

            def a_step(s, parity, i=None):
                tiles, rows, n = shape(s)
                act.wait_ge(s_a_tr, s + 1)
                at_least(act, s_xt, (s - 1) * GT)
                for k in range(KT):
                    last = nc.scalar.copy(x0T[:, parity, k, 0:n], bank[4 + 2 * parity + k][:, 0:n])
                last.then_inc(s_x0T, 1)
                xt_rows(s - 1, 1 - parity, i if i is None else (i if parity else i - 1))

            def xt_rows(s, parity, stored):
                if not exists(s):
                    return
                tiles, rows, _ = shape(s)
                at_least(act, s_table[parity], 32 * (s // 2 if stored is None else stored))
                for t in range(tiles):
                    act.wait_ge(s_xt, s * GT + t + 1)
                    nc.scalar.copy(xt_out[0:rows, parity, t, :], bank[t][0:rows, 0:ROW]).then_inc(s_xt_out, 1)

            steps(act, 4, a_step)
            xt_rows(FULL, FULL % 2, None)

            def b_exp(s):
                tiles, rows, _ = shape(s)
                act.wait_ge(s_score, s + 1)
                nc.scalar.activation(expo[0:rows, 0:tiles, :], shifted[0:rows, 0:tiles, :], ACT.Exp).then_inc(s_exp, 1)

            def b_split(s, parity):
                _, _, n = shape(s)
                act.wait_ge(s_b_tr, s + 1)
                at_least(act, s_h, (s - 1) * E * HALVES)
                for k in range(KT):
                    last = nc.scalar.activation(x2T_hi[:, parity, k, 0:n], bank[6 + k][:, 0:n], ACT.Copy, scale=SPLIT)
                last.then_inc(s_x2T_hi, 1)

            def b_logit_exp(s):
                tiles, rows, _ = shape(s)
                act.wait_ge(s_lshift, s + 1)
                nc.scalar.activation(logit_exp[0:rows, 0:tiles, :], logit_shifted[0:rows, 0:tiles, :],
                                     ACT.Exp).then_inc(s_lexp, 1)

            def b_combT(s, parity):
                _, _, n = shape(s)
                act.wait_ge(s_comb_tr, s + 1)
                if exists(s - 1):
                    act.wait_ge(s_y, item_done(s - 1, E))
                nc.scalar.copy(combT[:, parity, 0:n], bank[7][:].bitcast(fp16)[0:96, 0:n]).then_inc(s_combT, 1)

            def hidden(c, e):
                _, _, n = shape(c)
                q = c * E + e
                for f in range(HALVES):
                    act.wait_ge(s_h, q * HALVES + f + 1)
                    at_least(act, s_hlo, (q - 1) * HALVES)
                    nc.scalar.activation(h32[:, e % 2, f, 0:n], bank[2 * (e % 2) + f][:, 0:n], ACT.Gelu,
                                         bias=b1_col[:, e * HALVES + f:e * HALVES + f + 1],
                                         scale=UNSPLIT).then_inc(s_gelu, 1)
                pc, pe = before(c, e, RING_H)
                if exists(pc):
                    act.wait_ge(s_y, item_done(pc, pe))
                for f in range(HALVES):
                    act.wait_ge(s_gelu, q * HALVES + f + 1)
                    nc.scalar.activation(h_hi[:, e % RING_H, f, 0:n], h32[:, e % 2, f, 0:n], ACT.Copy,
                                         scale=SPLIT).then_inc(s_hhi, 1)

            def c_step(s, parity, i=None):
                c = s - 1
                for e in range(E):
                    if exists(c):
                        hidden(c, e)
                    if e == 0 and exists(c):
                        b_logit_exp(c)
                    if e == 0 and exists(s):
                        b_exp(s)
                    if e == 3 and exists(c):
                        b_combT(c, 1 - parity)
                    if e == 6 and exists(s):
                        b_split(s, parity)

            steps(act, 2, c_step, 1)

        @block.vector
        def _(dve):
            link = Chain(dve, setup_chain, 0)
            dve.wait_ge(s_const, 6)
            dve.wait_ge(s_w, 48)
            for n in range(2):
                for k in range(KT):
                    link(nc.vector.tensor_tensor(attn_prod[:], wext[:, k, 0:D].rearrange("p (h c) -> p h c", h=H),
                                                 attn[:, n, :, :], ALU.mult))
                    ins = nc.vector.tensor_reduce(wext[:, k, D + n * H:D + (n + 1) * H], attn_prod[:], X, ALU.add)
                    link(ins)
            dve.sem_inc(s_wext, 1)
            dve.wait_ge(s_small, 16 * 9)
            nc.vector.memset(rows_f[:], 0.0)
            link(nc.vector.memset(b2_parts[:], 0.0))
            for n in range(2):
                nc.vector.tensor_copy(rows_f[0:TILES, n, 0:TAIL_ROWS], rows_in[0:TILES, n, 0:TAIL_ROWS])
                nc.vector.tensor_copy(rows_f[0:TILES - 1, n, TAIL_ROWS:P], rows_in[0:TILES - 1, n, TAIL_ROWS:P])
            link(nc.vector.memset(b2_hi[:], 0.0))
            dve.sem_inc(s_rows_f, 1)
            for row in (0, 32, 64):
                last = nc.vector.tensor_scalar(b2_hi[row:row + E, :], b2_in[row:row + E, :], SPLIT, None, ALU.mult)
            link(last)
            for row in (0, 64):
                nc.vector.tensor_copy(b2_parts[row:row + E, :], b2_hi[row:row + E, :])
            link(nc.vector.scalar_tensor_tensor(out=b2_parts[32:32 + E, :], in0=b2_in[32:32 + E, :], scalar=SPLIT,
                                                in1=b2_hi[32:32 + E, :], op0=ALU.mult, op1=ALU.subtract))
            dve.wait_ge(s_setup_tr, 1)
            nc.vector.tensor_scalar(router64[:], bank[0][:, 0:KT * E].rearrange("p (k e) -> p k e", k=KT), SPLIT, None, ALU.mult)
            nc.vector.tensor_copy(b1_col[:], bank[0][:, 16:16 + E * HALVES])
            link(nc.vector.tensor_copy(index[:], bank[0][:, 64:64 + 2 * TILES].rearrange("p (n t) -> p n t", n=2)))
            link(nc.vector.tensor_copy(router_hi[:], router64[:]))
            nc.vector.tensor_tensor(router_lo[:], router64[:], router_hi[:], ALU.subtract).then_inc(s_setup, 1)

            def norm_stats(link, rows, tiles, get):
                settle(dve)
                for t in range(tiles):
                    last = nc.vector.bn_stats(stats[0:rows, t, :], get(t))
                link(last)
                settle(dve)
                for t in range(tiles):
                    last = nc.vector.bn_aggr(mean_var[0:rows, t, :], stats[0:rows, t, :])
                link(last)
                return nc.vector.tensor_scalar(var_eps[0:rows, 0:tiles], mean_var[0:rows, 0:tiles, 1], EPS, None, ALU.add)

            def norm_rstd(link, rows, tiles):
                r, n = rstd_0[0:rows, 0:tiles], newton[0:rows, 0:tiles]
                link(nc.vector.tensor_tensor(n, r, r, ALU.mult))
                link(nc.vector.tensor_tensor(n, n, var_eps[0:rows, 0:tiles], ALU.mult))
                link(nc.vector.tensor_scalar(n, n, -0.5, 1.5, ALU.mult, ALU.add))
                link(nc.vector.tensor_tensor(rstd[0:rows, 0:tiles], r, n, ALU.mult))

            def normed(dst, src, rows, t):
                return nc.vector.tensor_scalar(dst, src, mean_var[0:rows, t, 0:1], rstd[0:rows, t:t + 1],
                                               ALU.subtract, ALU.mult)

            link_a = Chain(dve, a_chain, 6)

            def a_step(s, parity, i=None):
                tiles, rows, _ = shape(s)
                link_a.step(s)
                dve.wait_ge(s_x[parity], nth(s, parity, i) * 16 + 16)
                xs = x_of(s)
                norm_stats(link_a, rows, tiles, lambda t: xs[:, t, :]).then_inc(s_a_var, 1)
                dve.wait_ge(s_a_pow, s + 1)
                norm_rstd(link_a, rows, tiles)
                at_least(dve, s_a_tr, s - 1)
                for t in range(tiles):
                    last = normed(x0[0:rows, parity, t, :], xs[:, t, :], rows, t)
                last.then_inc(s_x0, 1)

            steps(dve, 2, a_step)

            dve.wait_ge(s_experts, 32)
            for n in range(2):
                flat = "p e k n -> p (e k n)"
                link(nc.vector.tensor_scalar(w_hi[n][:].rearrange(flat), w_in[n][:].rearrange(flat), SPLIT, None, ALU.mult))
                last = nc.vector.scalar_tensor_tensor(out=w_lo[n][:].rearrange(flat), in0=w_in[n][:].rearrange(flat),
                                                      scalar=SPLIT, in1=w_hi[n][:].rearrange(flat),
                                                      op0=ALU.mult, op1=ALU.subtract)
            last.then_inc(s_experts_split, 1)

            link_b = Chain(dve, b_chain, 11)
            link_b2 = Chain(dve, b2_chain, 16)

            def b_scores(s, parity, i):
                tiles, rows, _ = shape(s)
                link_b.step(s)
                sl = (slice(0, rows), slice(0, tiles))
                dve.wait_ge(s_gather[parity], nth(s, parity, i) * (32 * GT) + 32 * tiles)
                link_b(nc.vector.tensor_tensor(score[sl], xg[0:rows, parity, 0:tiles, D:D + H],
                                               alg[0:rows, parity, 0:tiles, :], ALU.add))
                link_b(nc.vector.scalar_tensor_tensor(out=lrelu[sl], in0=score[sl], scalar=SLOPE, in1=score[sl],
                                                      op0=ALU.mult, op1=ALU.max))
                link_b(nc.vector.tensor_reduce(top[sl], lrelu[sl], X, ALU.max))
                nc.vector.tensor_tensor(shifted[sl], lrelu[sl], top[sl].unsqueeze(2).to_broadcast([rows, tiles, H]),
                                        ALU.subtract).then_inc(s_score, 1)

            def b_alpha(s):
                tiles, rows, _ = shape(s)
                sl = (slice(0, rows), slice(0, tiles))
                dve.wait_ge(s_exp, s + 1)
                link_b(nc.vector.tensor_reduce(total[sl], expo[sl], X, ALU.add))
                link_b(nc.vector.reciprocal(inverse[sl], total[sl]))
                nc.vector.tensor_tensor(alpha[sl], expo[sl], inverse[sl].unsqueeze(2).to_broadcast([rows, tiles, H]),
                                        ALU.mult).then_inc(s_alpha, 1)

            def b_message(s):
                tiles, rows, _ = shape(s)
                sl = (slice(0, rows), slice(0, tiles))
                dve.wait_ge(s_prod, s + 1)
                nc.vector.tensor_reduce(tmp[sl], prod[sl].rearrange("p t h c -> p t c h"), X, ALU.add).then_inc(s_tmp, 1)

            def b_stats(s):
                tiles, rows, _ = shape(s)
                xs = x_of(s)
                dve.wait_ge(s_x1, s + 1)
                norm_stats(link_b, rows, tiles, lambda t: xs[:, t, :]).then_inc(s_b_var, 1)

            def b_norm(s):
                tiles, rows, _ = shape(s)
                xs = x_of(s)
                dve.wait_ge(s_b_pow, s + 1)
                norm_rstd(link_b, rows, tiles)
                at_least(dve, s_b_tr, s)
                at_least(dve, s_acc0, s)
                for t in range(tiles):
                    last = normed(x2[0:rows, t, :], xs[:, t, :], rows, t)
                last.then_inc(s_x2, 1)

            def b_split(s, parity):
                tiles, rows, n = shape(s)
                dve.wait_ge(s_x2T_hi, s + 1)
                for k in range(KT):
                    last = nc.vector.scalar_tensor_tensor(out=x2T_lo[:, parity, k, 0:n], in0=bank[6 + k][:, 0:n], scalar=SPLIT,
                                                          in1=x2T_hi[:, parity, k, 0:n], op0=ALU.mult, op1=ALU.subtract)
                last.then_inc(s_x2T_lo, 1)

            def b_logits(s):
                tiles, rows, _ = shape(s)
                sl = (slice(0, rows), slice(0, tiles))
                link_b2.step(s)
                dve.wait_ge(s_logits, s + 1)
                link_b2(nc.vector.tensor_scalar(logits[sl], bank[6][0:rows, 0:tiles * E].rearrange("p (t e) -> p t e", e=E),
                                                UNSPLIT, None, ALU.mult))
                link_b2(nc.vector.tensor_reduce(logit_top[sl], logits[sl], X, ALU.max))
                nc.vector.tensor_tensor(logit_shifted[sl], logits[sl], logit_top[sl].unsqueeze(2).to_broadcast([rows, tiles, E]),
                                        ALU.subtract).then_inc(s_lshift, 1)

            def b_best(s):
                tiles, rows, _ = shape(s)
                sl = (slice(0, rows), slice(0, tiles))
                wide = [rows, tiles, E]
                dve.wait_ge(s_lexp, s + 1)
                link_b2(nc.vector.tensor_reduce(prob_total[sl], logit_exp[sl], X, ALU.add))
                link_b2(nc.vector.reciprocal(prob_inverse[sl], prob_total[sl]))
                link_b2(nc.vector.tensor_tensor(prob[sl], logit_exp[sl], prob_inverse[sl].unsqueeze(2).to_broadcast(wide), ALU.mult))
                settle(dve)
                for t in range(tiles):
                    last = nc.vector.max(best[0:rows, t, :], prob[0:rows, t, :])
                link_b2(last)
                settle(dve)
                for t in range(tiles):
                    last = nc.vector.max_index(best_index[0:rows, t, :], best[0:rows, t, :], prob[0:rows, t, :])
                link_b2(last)

            def b_route(s, parity):
                tiles, rows, _ = shape(s)
                sl = (slice(0, rows), slice(0, tiles))
                wide = [rows, tiles, E]
                link_b2(nc.vector.tensor_copy(best_f[sl], best_index[0:rows, 0:tiles, 0:TOP_K]))
                for n in range(TOP_K):
                    last = nc.vector.tensor_tensor(mask[0:rows, n, 0:tiles, :], iota8[0:rows].unsqueeze(1).to_broadcast(wide),
                                                   best_f[0:rows, 0:tiles, n:n + 1].to_broadcast(wide), ALU.is_equal)
                link_b2(last)
                link_b2(nc.vector.tensor_tensor(mask[0:rows, 0, 0:tiles, :], mask[0:rows, 0, 0:tiles, :],
                                                mask[0:rows, 1, 0:tiles, :], ALU.add))
                link_b2(nc.vector.tensor_tensor(kept[sl], mask[0:rows, 0, 0:tiles, :], prob[sl], ALU.mult))
                link_b2(nc.vector.tensor_reduce(prob_total[sl], kept[sl], X, ALU.add))
                link_b2(nc.vector.tensor_scalar(prob_total[sl], prob_total[sl], 1e-12, None, ALU.max))
                link_b2(nc.vector.reciprocal(prob_inverse[sl], prob_total[sl]))
                link_b2(nc.vector.scalar_tensor_tensor(out=comb64[sl], in0=kept[sl], scalar=SPLIT,
                                                       in1=prob_inverse[sl].unsqueeze(2).to_broadcast(wide),
                                                       op0=ALU.mult, op1=ALU.mult))
                at_least(dve, s_comb_tr, s)
                nc.vector.tensor_copy(comb_parts[0:rows, 0:tiles, 0:E], comb64[sl])
                nc.vector.tensor_copy(comb_parts[0:rows, 0:tiles, 32:32 + E], comb64[sl])
                link_b2(nc.vector.tensor_scalar(comb[0:rows, parity, 0:tiles, :], comb64[sl], UNSPLIT / SPLIT, None, ALU.mult))
                nc.vector.tensor_tensor(comb_parts[0:rows, 0:tiles, 64:64 + E], comb64[sl], comb_parts[0:rows, 0:tiles, 0:E],
                                        ALU.subtract).then_inc(s_comb, 1)

            def remainder(c, e):
                _, _, n = shape(c)
                q = c * E + e
                for f in range(HALVES):
                    dve.wait_ge(s_hhi, q * HALVES + f + 1)
                    nc.vector.scalar_tensor_tensor(out=h_lo[:, e % RING_H, f, 0:n], in0=h32[:, e % 2, f, 0:n], scalar=SPLIT,
                                                   in1=h_hi[:, e % RING_H, f, 0:n], op0=ALU.mult,
                                                   op1=ALU.subtract).then_inc(s_hlo, 1)

            def accumulate(c, j, parity):
                tiles, rows, _ = shape(c)
                if j == 0:
                    dve.wait_ge(s_acc0, c + 1)
                for b in range(-(-tiles // 2)):
                    u = uses(c, j, b)
                    dve.wait_ge(s_y, u)
                    at_least(dve, s_acc, u - (2 if tiles > 1 else 1))
                    y = bank[4 + (b if tiles > 1 else j % 2)]
                    for t in range(2 * b, min(tiles, 2 * b + 2)):
                        a = acc[0:rows, parity, t, :]
                        weight_of = UNSPLIT if j == E else comb[0:rows, parity, t, j:j + 1]
                        last = nc.vector.scalar_tensor_tensor(out=a, in0=y[0:rows, (t % 2) * D:(t % 2 + 1) * D], scalar=weight_of,
                                                              in1=a, op0=ALU.mult, op1=ALU.add)
                    last.then_inc(s_acc, 1)

            def finish(c, e, parity):
                pc, pe = before(c, e, LAG)
                own = parity if e >= LAG else 1 - parity
                if exists(pc):
                    accumulate(pc, pe, own)
                    if pe == E - 1:
                        accumulate(pc, E, own)

            def c_step(s, parity, i=None):
                c = s - 1
                for e in range(E):
                    if exists(c):
                        if e == 0:
                            b_logits(c)
                        if e == 2:
                            b_route(c, 1 - parity)
                    if exists(s):
                        if e == 0:
                            b_scores(s, parity, i)
                        if e == 1:
                            b_alpha(s)
                        if e == 3:
                            b_message(s)
                        if e == 4:
                            b_stats(s)
                        if e == 5:
                            b_norm(s)
                        if e == 7:
                            b_split(s, parity)
                    if exists(c):
                        if e == 1:
                            b_best(c)
                        remainder(c, e)
                        finish(c, e, 1 - parity)

            steps(dve, 2, c_step, 1)
            for e in range(LAG):
                finish(FULL + 1, e, (FULL + 1) % 2)

        @block.tensor
        def _(pe):
            pe.wait_ge(s_const, 6)
            pe.wait_ge(s_small, 16 * 9)
            pe.wait_ge(s_rows_f, 1)
            for k in range(KT):
                nc.tensor.transpose(bank[0][:, k * E:(k + 1) * E], router_in[:, k * P:(k + 1) * P], ident[0:E, 0:E])
            nc.tensor.transpose(bank[0][:, 16:16 + E * HALVES], b1_in[:], ident[0:E * HALVES, 0:E * HALVES])
            for n in range(2):
                last = nc.tensor.transpose(bank[0][:, 64 + n * TILES:64 + (n + 1) * TILES], rows_f[:, n, :],
                                           ident[0:TILES, 0:TILES])
            last.then_inc(s_setup_tr, 1)
            pe.wait_ge(s_setup, 1)
            pe.wait_ge(s_wext, 1)

            def a_step(s, parity, i=None):
                tiles, rows, _ = shape(s)
                pe.wait_ge(s_x0, s + 1)
                at_least(pe, s_x0T, s - 1)
                for k in range(KT):
                    for t in range(tiles):
                        last = nc.tensor.transpose(bank[4 + 2 * parity + k][:, t * P:t * P + rows],
                                                   x0[0:rows, parity, t, k * P:(k + 1) * P], ident[0:rows, 0:rows])
                last.then_inc(s_a_tr, 1)
                xt_product(s - 1, 1 - parity)

            def xt_product(s, parity):
                if not exists(s):
                    return
                tiles, rows, _ = shape(s)
                pe.wait_ge(s_x0T, s + 1)
                for t in range(tiles):
                    at_least(pe, s_xt_out, (s - 1) * GT + t + 1)
                    for k in range(KT):
                        last = nc.tensor.matmul(bank[t][0:rows, 0:ROW], x0T[:, parity, k, t * P:t * P + rows], wext[:, k, :],
                                                start=(k == 0), stop=(k == KT - 1))
                    last.then_inc(s_xt, 1)

            steps(pe, 4, a_step)
            xt_product(FULL, FULL % 2)

            def b_transpose(s):
                tiles, rows, _ = shape(s)
                pe.wait_ge(s_x2, s + 1)
                at_least(pe, s_lshift, s)
                at_least(pe, s_combT, s)
                for k in range(KT):
                    for t in range(tiles):
                        last = nc.tensor.transpose(bank[6 + k][:, t * P:t * P + rows], x2[0:rows, t, k * P:(k + 1) * P],
                                                   ident[0:rows, 0:rows])
                last.then_inc(s_b_tr, 1)

            def b_router(s, parity):
                tiles, rows, _ = shape(s)
                pe.wait_ge(s_x2T_lo, s + 1)
                for t in range(tiles):
                    parts = [(x, w, k) for k in range(KT)
                             for x, w in ((x2T_hi, router_hi), (x2T_hi, router_lo), (x2T_lo, router_hi))]
                    for n, (xp, wp, k) in enumerate(parts):
                        last = nc.tensor.matmul(bank[6][0:rows, t * E:(t + 1) * E], xp[:, parity, k, t * P:t * P + rows], wp[:, k, :],
                                                start=(n == 0), stop=(n == len(parts) - 1))
                last.then_inc(s_logits, 1)

            def b_combine(s):
                tiles, rows, _ = shape(s)
                pe.wait_ge(s_comb, s + 1)
                for t in range(tiles):
                    last = nc.tensor.transpose(bank[7][:].bitcast(fp16)[0:96, t * P:t * P + rows], comb_parts[0:rows, t, :],
                                               ident16[0:rows, 0:rows])
                last.then_inc(s_comb_tr, 1)

            def first(c, e, parity):
                _, _, n = shape(c)
                q = c * E + e
                for f in range(HALVES):
                    at_least(pe, s_gelu, (q - 2) * HALVES + f + 1)
                    parts = [(w, x, k) for k in range(KT)
                             for w, x in ((w_hi[0], x2T_hi), (w_hi[0], x2T_lo), (w_lo[0], x2T_hi))]
                    for m, (wp, xp, k) in enumerate(parts):
                        last = nc.tensor.matmul(bank[2 * (e % 2) + f][:, 0:n], wp[:, e, k, f * P:(f + 1) * P],
                                                xp[:, parity, k, 0:n], start=(m == 0), stop=(m == len(parts) - 1))
                    last.then_inc(s_h, 1)

            def bias(c, parity):
                pe.wait_ge(s_combT, c + 1)
                output(c, E, lambda t, rows: [(combT[:, parity, t * P:t * P + rows], b2_parts[:])])

            def second(c, e):
                pe.wait_ge(s_hlo, (c * E + e + 1) * HALVES)
                r = e % RING_H
                output(c, e, lambda t, rows: [
                    (hp[:, r, f, t * P:t * P + rows], wp[:, e, f, :]) for f in range(HALVES)
                    for hp, wp in ((h_hi, w_hi[1]), (h_hi, w_lo[1]), (h_lo, w_hi[1]))])

            def output(c, j, parts_of):
                tiles, rows, _ = shape(c)
                for b in range(-(-tiles // 2)):
                    u = uses(c, j, b)
                    at_least(pe, s_acc, u - 2)
                    y = bank[4 + (b if tiles > 1 else j % 2)]
                    for t in range(2 * b, min(tiles, 2 * b + 2)):
                        parts = parts_of(t, rows)
                        for m, (lhsT, rhs) in enumerate(parts):
                            last = nc.tensor.matmul(y[0:rows, (t % 2) * D:(t % 2 + 1) * D], lhsT, rhs,
                                                    start=(m == 0), stop=(m == len(parts) - 1))
                    last.then_inc(s_y, 1)

            def seconds(c, e, parity):
                pc, pe_ = before(c, e, LAG)
                if exists(pc):
                    second(pc, pe_)
                    if pe_ == E - 1:
                        bias(pc, 1 - parity)

            pe.wait_ge(s_experts_split, 1)

            def c_step(s, parity, i=None):
                c = s - 1
                for e in range(E):
                    if exists(c):
                        first(c, e, 1 - parity)
                        if e == 3:
                            b_combine(c)
                    if exists(s):
                        if e == 6:
                            b_transpose(s)
                        if e == 7:
                            b_router(s, parity)
                    if exists(c):
                        seconds(c, e, 1 - parity)

            steps(pe, 2, c_step, 1)
            for e in range(LAG):
                seconds(FULL + 1, e, (FULL + 1) % 2)


_INS = ['x', 'src', 'dst', 'L0_gnn_weight', 'L0_gnn_attn_l', 'L0_gnn_attn_r', 'L0_ffn_router_w', 'L0_ffn_w1',
        'L0_ffn_b1', 'L0_ffn_w2', 'L0_ffn_b2']
_OUTS = [((N, D), 'float32')]


def kernel(**inputs):
    import numpy as _np
    import concourse.bacc as _bacc
    from concourse import mybir as _mybir
    from concourse.bass_utils import run_bass_kernel_spmd as _run

    nc = _bacc.Bacc("TRN2", target_bir_lowering=False, num_devices=1)
    arrays, args = {}, []
    for name in _INS:
        a = _np.ascontiguousarray(inputs[name])
        arrays[f"in_{name}_dram"] = a
        args.append(nc.dram_tensor(f"in_{name}_dram", a.shape, _mybir.dt.from_np(a.dtype), kind="ExternalInput").ap())
    for i, (shape, dtype) in enumerate(_OUTS):
        dt = _mybir.dt.from_np(_np.dtype(dtype))
        args.append(nc.dram_tensor(f"out_{i}_dram", shape, dt, kind="ExternalOutput").ap())
    build(nc, *args)
    r = _run(nc, [arrays], core_ids=[0])
    got = tuple(r.results[0][f"out_{i}_dram"] for i in range(len(_OUTS)))
    return got[0]
```

```python
import concourse.bass as bass
from concourse import mybir
from contextlib import ExitStack

N, D, H, C, E, TOP_K = 6250, 256, 4, 64, 8, 2
P = 128
KT = D // P
GT = 4
GROUP = GT * P
FULL = N // GROUP
TILES = -(-N // P)
TAIL_ROWS = N - FULL * GROUP
STEPS = FULL + 1
ROW = D + 2 * H
EPS = 1e-5
SLOPE = 0.01
SPLIT = 64.0
UNSPLIT = 1.0 / (SPLIT * SPLIT)
H_SPLIT = 8.0
H_UNSPLIT = 1.0 / (H_SPLIT * SPLIT)
HALVES = 2
USES = 2 * (E + 1)
RING_H = 4
H_WORDS = RING_H * HALVES * GROUP
SPLIT_HI, SPLIT_LO = 4, 6
LAG = 2

assert TAIL_ROWS <= P and TILES == FULL * GT + 1 and FULL % 2 == 0


def build(nc, x, src, dst, weight, attn_l, attn_r, router_w, w1, b1, w2, b2, out):
    fp32, fp16 = mybir.dt.float32, mybir.dt.float16
    i32, u32 = mybir.dt.int32, mybir.dt.uint32
    ALU = mybir.AluOpType
    ACT = mybir.ActivationFunctionType
    X = mybir.AxisListType.X

    table = nc.dram_tensor("xt_table", (N, ROW), fp32, kind="Internal").ap()
    al_table = nc.dram_tensor("al_table", (N, H), fp32, kind="Internal").ap()

    ctx = ExitStack()
    with ctx:
        def sb(name, shape, dt=fp32):
            return ctx.enter_context(nc.sbuf_tensor(name, shape, dt))

        def sem(name):
            return ctx.enter_context(nc.semaphore(name))

        def pair(name):
            return [sem(f"{name}{i}") for i in range(2)]

        bank = [ctx.enter_context(nc.psum_tensor(f"bank{i}", [P, 512], fp32)) for i in range(8)]

        ident = sb("ident", [P, P])
        ident16 = sb("ident16", [P, P], fp16)
        iota8 = sb("iota8", [P, E])
        minus_half = sb("minus_half", [P, GT])
        wext = sb("wext", [P, KT, ROW])
        attn = sb("attn", [P, 2, H, C])
        attn_prod = sb("attn_prod", [P, KT, H, C])
        rows_in = sb("rows_in", [TILES, 2, P], i32)
        rows_f = sb("rows_f", [TILES, 2, P])
        index = sb("index", [P, 2, TILES], u32)
        index_now = sb("index_now", [P, 2, 2, GT], u32)
        router_in = sb("router_in", [E, D])
        router64 = sb("router64", [P, KT, E])
        router_hi = sb("router_hi", [P, KT, E], fp16)
        router_lo = sb("router_lo", [P, KT, E], fp16)
        b1_in = sb("b1_in", [E * HALVES, P])
        b1_col = sb("b1_col", [P, E * HALVES])
        b2_in = sb("b2_in", [96, D])
        b2_hi = sb("b2_hi", [96, D], fp16)
        b2_parts = sb("b2_parts", [96, D], fp16)
        w_in = [sb(f"w{n}_in", [P, E, KT, D]) for n in (1, 2)]
        w_hi = [sb(f"w{n}_hi", [P, E, KT, D], fp16) for n in (1, 2)]
        w_lo = [sb(f"w{n}_lo", [P, E, KT, D], fp16) for n in (1, 2)]
        x_all = sb("x_all", [P, TILES, D])
        stats = sb("stats", [P, GT, 6])
        mean_var = sb("mean_var", [P, 2, GT, 2])
        var_eps = sb("var_eps", [P, 2, GT])
        rstd_0 = sb("rstd_0", [P, 2, GT])
        newton = sb("newton", [P, 2, GT])
        rstd = sb("rstd", [P, 2, GT])
        x0 = sb("x0", [P, 2, GT, D])
        x0T = sb("x0T", [P, 2, KT, GROUP])
        xt_out = sb("xt_out", [P, 2, GT, ROW])
        xg = sb("xg", [P, 2, GT, ROW])
        alg = sb("alg", [P, 2, GT, H])
        score = sb("score", [P, GT, H])
        lrelu = sb("lrelu", [P, GT, H])
        top = sb("top", [P, GT])
        shifted = sb("shifted", [P, GT, H])
        expo = sb("expo", [P, GT, H])
        total = sb("total", [P, GT])
        inverse = sb("inverse", [P, GT])
        alpha = sb("alpha", [P, GT, H])
        prod = sb("prod", [P, GT, H, C])
        tmp = sb("tmp", [P, GT, C])
        x2 = sb("x2", [P, GT, D])
        x2T_hi = sb("x2T_hi", [P, 2, KT, GROUP], fp16)
        x2T_lo = sb("x2T_lo", [P, 2, KT, GROUP], fp16)
        logits = sb("logits", [P, GT, E])
        logit_top = sb("logit_top", [P, GT])
        logit_shifted = sb("logit_shifted", [P, GT, E])
        logit_exp = sb("logit_exp", [P, GT, E])
        prob_total = sb("prob_total", [P, GT])
        prob_inverse = sb("prob_inverse", [P, GT])
        prob = sb("prob", [P, GT, E])
        best = sb("best", [P, GT, 8])
        best_index = sb("best_index", [P, GT, 8], u32)
        best_f = sb("best_f", [P, GT, TOP_K])
        mask = sb("mask", [P, 2, GT, E])
        kept = sb("kept", [P, GT, E])
        comb = sb("comb", [P, 2, GT, E])
        comb64 = sb("comb64", [P, GT, E])
        comb_parts = sb("comb_parts", [P, GT, 96], fp16)
        combT = sb("combT", [96, 2, GROUP], fp16)
        acc = sb("acc", [P, 2, GT, D])
        h32 = sb("h32", [P, 2, HALVES, GROUP])
        h_hi, h_lo = [w_in[0][:].rearrange("p e k n -> p (e k n)").bitcast(fp16)[:, n * H_WORDS:(n + 1) * H_WORDS].rearrange(
            "p (r f n) -> p r f n", r=RING_H, f=HALVES) for n in range(2)]

        s_settled = sem("waits_settled")
        s_w = sem("gnn_weights_loaded")
        s_small = sem("small_inputs_loaded")
        s_experts = pair("expert_weights_loaded")
        s_const = sem("constants_made")
        s_rows_f = sem("edge_rows_as_float")
        s_setup_tr = sem("setup_transposed")
        s_setup = sem("setup_evacuated")
        s_wext = sem("wext_made")
        s_split_hi = sem("expert_weights_hi")
        s_experts_split = sem("expert_weights_split")
        setup_chain = sem("setup_chain")
        s_x = pair("x_loaded")
        s_a_var = sem("a_var_ready")
        s_a_pow = sem("a_power_ready")
        s_a_rstd = sem("a_rstd_ready")
        s_x0 = sem("x0_ready")
        s_a_tr = sem("x0_transposed")
        s_x0T = sem("x0T_in_sbuf")
        s_xt = sem("xt_tile_done")
        s_xt_out = sem("xt_tile_in_sbuf")
        s_table = pair("table_rows_stored")
        a_chain = sem("a_chain")
        a_rstd_chain = sem("a_rstd_chain")
        s_index = sem("index_picked")
        s_gather = pair("rows_gathered")
        s_score = sem("scores_ready")
        s_exp = sem("scores_exp")
        s_alpha = sem("alpha_ready")
        s_prod = sem("rows_weighted")
        s_tmp = sem("message_ready")
        s_x1 = sem("x1_ready")
        s_b_var = sem("b_var_ready")
        s_b_pow = sem("b_power_ready")
        s_x2 = sem("x2_ready")
        s_b_tr = sem("x2_transposed")
        s_x2T_hi = sem("x2T_hi_ready")
        s_x2T_lo = sem("x2T_lo_ready")
        s_acc0 = sem("residual_ready")
        s_logits = sem("logits_done")
        s_lshift = sem("logits_shifted")
        s_lexp = sem("logits_exp")
        s_comb = sem("combine_ready")
        s_comb_tr = sem("combine_transposed")
        s_combT = sem("combT_ready")
        b_chain = sem("b_chain")
        b2_chain = sem("b2_chain")
        s_h = sem("first_product_done")
        s_gelu = sem("gelu_done")
        s_hhi = sem("h_hi_ready")
        s_hlo = sem("h_lo_ready")
        s_y = sem("second_product_done")
        s_acc = sem("accumulated")
        s_out = pair("out_stored")

        def settle(eng):
            eng.sem_inc(s_settled, 1)

        def at_least(eng, s, count):
            if not isinstance(count, int) or count > 0:
                eng.wait_ge(s, count)

        class Chain:

            def __init__(self, eng, s, per_step):
                self.eng, self.s, self.per_step, self.base, self.k = eng, s, per_step, 0, 0

            def step(self, s):
                assert self.k in (0, self.per_step), self.k
                self.base, self.k = s * self.per_step, 0

            def __call__(self, ins):
                self.k += 1
                ins.then_inc(self.s, 1)
                self.eng.wait_ge(self.s, self.base + self.k)

        def is_tail(s):
            return isinstance(s, int) and s == 0

        def shape(s):
            return (1, TAIL_ROWS, TAIL_ROWS) if is_tail(s) else (GT, P, GROUP)

        def first_tile(s):
            return TILES - 1 if is_tail(s) else (s - 1) * GT

        def tiles_before(s):
            return 0 if is_tail(s) else 1 + (s - 1) * GT

        def tokens_of(ap, s):
            tiles, rows, n = shape(s)
            return ap[bass.ds(first_tile(s) * P, n), :].rearrange("(t p) d -> p t d", p=rows)

        def x_of(s):
            tiles, rows, _ = shape(s)
            return x_all[0:rows, bass.ds(first_tile(s), tiles), :]

        def uses(c, j, b):
            return j + 1 if is_tail(c) else (c - 1) * USES + E + 1 + 2 * j + b + 1

        def item_done(c, j):
            return uses(c, j, 0 if is_tail(c) else 1)

        def output_bank(c, j, b):
            if j == E:
                return bank[6 + b]
            return bank[4 + (j % 2 if is_tail(c) else b)]

        def bank_added(c, j, b):
            if is_tail(c):
                return uses(c, j - 2, b)
            if j > 0:
                return uses(c, j - 1, b)
            return uses(0, E - 2 + b, 0) if isinstance(c, int) and c == 1 else uses(c - 1, E - 1, b)

        def before(c, e, back):
            return (c, e - back) if e >= back else (c - 1, e - back + E)

        def exists(c):
            return not isinstance(c, int) or 0 <= c <= FULL

        def steps(eng, first, body, extra=0):
            for s in range(first):
                body(s, s % 2)
            with eng.Fori(first // 2, FULL // 2) as i:
                for parity in range(2):
                    body(i * 2 + parity, parity, i)
            for s in range(FULL, FULL + 1 + extra):
                body(s, s % 2)

        def by_vector(s):
            return isinstance(s, int) and s < 2

        def weighted_rows(engine, s, parity):
            tiles, rows, _ = shape(s)
            sl = (slice(0, rows), slice(0, tiles))
            return engine.tensor_tensor(prod[sl], xg[0:rows, parity, 0:tiles, 0:D].rearrange("p t (h c) -> p t h c", h=H),
                                        alpha[sl].unsqueeze(3).to_broadcast([rows, tiles, H, C]), ALU.mult)

        def add_message(engine, s):
            tiles, rows, _ = shape(s)
            xh = x_of(s).rearrange("p t (h c) -> p t h c", h=H)
            return engine.tensor_tensor(xh, xh, tmp[0:rows, 0:tiles].unsqueeze(2).to_broadcast([rows, tiles, H, C]), ALU.add)

        def nth(s, parity, i):
            return s // 2 if i is None else i

        block = ctx.enter_context(nc.Block())

        @block.sync
        def _(sp):
            def a_step(s, parity, i=None):
                at_least(sp, s_x[parity], nth(s, parity, i) * 16)
                settle(sp)
                at_least(sp, s_x0, s - 3)
                settle(sp)
                sp.dma_start(x_of(s), tokens_of(x, s)).then_inc(s_x[parity], 16)
                if i is None and s == 2:
                    edge_rows()
                if i is not None or SPLIT_HI <= s < FULL:
                    expert_weights(s - SPLIT_HI, parity, 0 if i is None else i - SPLIT_HI // 2)

            def edge_rows():
                sp.dma_start(rows_in[:, 0, :][0:TILES - 1], dst[0:FULL * GROUP].rearrange("(t p) -> t p", p=P)).then_inc(s_small, 16)
                sp.dma_start(rows_in[TILES - 1:TILES, 0, 0:TAIL_ROWS], dst[FULL * GROUP:N].rearrange("(t p) -> t p", t=1)).then_inc(s_small, 16)
                sp.dma_start(rows_in[:, 1, :][0:TILES - 1], src[0:FULL * GROUP].rearrange("(t p) -> t p", p=P)).then_inc(s_small, 16)
                sp.dma_start(rows_in[TILES - 1:TILES, 1, 0:TAIL_ROWS], src[FULL * GROUP:N].rearrange("(t p) -> t p", t=1)).then_inc(s_small, 16)

            def expert_weights(e, parity, loaded):
                at_least(sp, s_experts[parity], 32 * loaded)
                for n, w in ((0, w1), (1, w2)):
                    sp.dma_start(w_in[n][:, bass.ds(e, 1), :, :].rearrange("p e k n -> p (e k) n"),
                                 w[bass.ds(e, 1), :, :].rearrange("e (k p) n -> p (e k) n", p=P)).then_inc(s_experts[parity], 16)

            steps(sp, SPLIT_HI + 2, a_step)

            def c_step(s, parity, i=None):
                c = s - 2
                if exists(c):
                    put(c, parity)

            def put(c, parity):
                tiles, rows, _ = shape(c)
                halves = [(0, GT // 2, 0), (GT // 2, GT, 1)] if isinstance(c, int) and c == FULL else [(0, tiles, 0 if is_tail(c) else 1)]
                for begin, end, b in halves:
                    sp.wait_ge(s_acc, uses(c, E, b))
                    sp.dma_start(tokens_of(out, c)[:, begin:end, :], acc[0:rows, parity, begin:end, :]).then_inc(s_out[parity], 16)

            steps(sp, 4, c_step, 2)
            sp.wait_ge(s_out[FULL % 2], 16 * (FULL // 2 + 2))
            sp.wait_ge(s_out[1 - FULL % 2], 16 * (STEPS // 2))

        @block.gpsimd
        def _(pool):
            nc.gpsimd.memset(ident[:], 1.0).then_inc(s_const, 1)
            pool.wait_ge(s_const, 1)
            nc.gpsimd.affine_select(out=ident[:], in_=ident[:], compare_op=ALU.is_equal, fill=0.0, base=0,
                                    pattern=[[-1, P]], channel_multiplier=1).then_inc(s_const, 1)
            pool.wait_ge(s_const, 2)
            nc.gpsimd.tensor_copy(ident16[:], ident[:]).then_inc(s_const, 1)
            nc.gpsimd.iota(iota8[:], pattern=[[1, E]], base=0, channel_multiplier=0,
                           allow_small_or_imprecise_dtypes=True).then_inc(s_const, 1)
            nc.gpsimd.memset(minus_half[:], -0.5).then_inc(s_const, 1)
            nc.gpsimd.memset(comb_parts[:], 0.0).then_inc(s_const, 1)
            pool.wait_ge(s_const, 6)

            def power(s, v, ready, done):
                tiles, rows, _ = shape(s)
                pool.wait_ge(ready, s + 1)
                nc.gpsimd.tensor_tensor(rstd_0[0:rows, v, 0:tiles], var_eps[0:rows, v, 0:tiles],
                                        minus_half[0:rows, 0:tiles], ALU.pow).then_inc(done, 1)

            def a_step(s, parity, i=None):
                tiles, rows, _ = shape(s)
                pool.wait_ge(s_a_var, s + 1)
                at_least(pool, s_a_tr, s - 1)
                settle(pool)
                nc.gpsimd.tensor_tensor(x0[0:rows, parity, 0:tiles, :], x_of(s),
                                        mean_var[0:rows, parity, 0:tiles, 0:1].to_broadcast([rows, tiles, D]),
                                        ALU.subtract).then_inc(s_x0, 1)
                at_least(pool, s_a_rstd, s - 1)
                power(s, parity, s_a_var, s_a_pow)

            steps(pool, 2, a_step)

            pool.wait_ge(s_table[0], 32 * ((STEPS + 1) // 2))
            pool.wait_ge(s_table[1], 32 * (STEPS // 2))
            pool.wait_ge(s_setup, 1)

            def gather(s, parity, begin, end):
                tiles, rows, _ = shape(s)
                if begin == 0:
                    at_least(pool, s_prod, s - 1)
                    nc.gpsimd.tensor_copy(index_now[0:rows, parity, :, 0:tiles],
                                          index[0:rows, :, bass.ds(first_tile(s), tiles)]).then_inc(s_index, 1)
                    pool.wait_ge(s_index, s + 1)
                    settle(pool)
                for t in range(begin, min(end, tiles)):
                    nc.gpsimd.indirect_dma_start(
                        out=xg[0:rows, parity, t, :], out_offset=None, in_=table,
                        in_offset=bass.IndirectOffsetOnAxis(ap=index_now[0:rows, parity, 0, t:t + 1], axis=0),
                    ).then_inc(s_gather[parity], 16)
                    nc.gpsimd.indirect_dma_start(
                        out=alg[0:rows, parity, t, :], out_offset=None, in_=al_table,
                        in_offset=bass.IndirectOffsetOnAxis(ap=index_now[0:rows, parity, 1, t:t + 1], axis=0),
                    ).then_inc(s_gather[parity], 16)

            def b_step(s, parity, i=None):
                cuts = (3, 3, GT) if i is None and s == 1 else (0, 0, GT) if i is None and s == 2 else (GT, GT, GT)
                portion = [(0, cuts[0]), (cuts[0], cuts[1]), (cuts[1], cuts[2])]

                def next_rows(n):
                    begin, end = portion[n]
                    if exists(s) and begin < end:
                        gather(s, parity, begin, end)

                next_rows(0)
                if exists(s - 1):
                    message(s - 1, 1 - parity)
                    next_rows(1)
                    power(s - 1, 0, s_b_var, s_b_pow)
                    next_rows(2)
                    residual(s - 1, 1 - parity, (s - 1) // 2 if i is None else (i if parity else i - 1))

            def message(s, parity):
                if by_vector(s):
                    return
                pool.wait_ge(s_alpha, s + 1)
                weighted_rows(nc.gpsimd, s, parity).then_inc(s_prod, 1)
                pool.wait_ge(s_tmp, s + 1)
                settle(pool)
                add_message(nc.gpsimd, s).then_inc(s_x1, 1)

            def residual(s, parity, before_it):
                tiles, rows, _ = shape(s)
                pool.wait_ge(s_x2, s + 1)
                pool.wait_ge(s_x1, s + 1)
                if exists(s - 2):
                    pool.wait_ge(s_out[parity], 16 * before_it)
                settle(pool)
                nc.gpsimd.tensor_tensor(acc[0:rows, parity, 0:tiles, :], x_of(s), x2[0:rows, 0:tiles, :],
                                        ALU.add).then_inc(s_acc0, 1)

            steps(pool, 4, b_step, 1)

        @block.scalar
        def _(act):
            act.dma_start(wext[:, :, 0:D], weight.rearrange("(k p) n -> p k n", p=P)).then_inc(s_w, 16)
            for n, a in ((0, attn_r), (1, attn_l)):
                act.dma_start(attn[:, n, :, :], a.partition_broadcast(P)).then_inc(s_w, 16)
            act.dma_start(router_in[:], router_w).then_inc(s_small, 16)
            act.dma_start(b1_in[:], b1.rearrange("e (h f) -> (e h) f", h=HALVES)).then_inc(s_small, 16)
            for row in (0, 32, 64):
                act.dma_start(b2_in[row:row + E, :], b2).then_inc(s_small, 16)

            def a_step(s, parity, i=None):
                tiles, rows, n = shape(s)
                if i is not None:
                    split_expert(s - SPLIT_HI, parity, i - SPLIT_HI // 2 + 1)
                act.wait_ge(s_a_tr, s + 1)
                if exists(s - 2):
                    act.wait_ge(s_xt, tiles_before(s - 1))
                for k in range(KT):
                    last = nc.scalar.copy(x0T[:, parity, k, 0:n], bank[4 + 2 * parity + k][:, 0:n])
                last.then_inc(s_x0T, 1)
                store(s - 2, parity)
                xt_rows(s - 1, 1 - parity, i if i is None else (i if parity else i - 1))

            def split_expert(e, parity, loaded):
                act.wait_ge(s_experts[parity], 32 * loaded)
                for n in range(2):
                    w, hi = (a[n][:, bass.ds(e, 1), :, :] for a in (w_in, w_hi))
                    last = nc.scalar.activation(hi, w, ACT.Copy, scale=SPLIT)
                last.then_inc(s_split_hi, 1)

            def xt_rows(s, parity, stored):
                if not exists(s):
                    return
                tiles, rows, _ = shape(s)
                at_least(act, s_table[parity], 32 * (s // 2 if stored is None else stored))
                act.wait_ge(s_a_rstd, s + 1)
                for t in range(tiles):
                    act.wait_ge(s_xt, tiles_before(s) + t + 1)
                    nc.scalar.activation(xt_out[0:rows, parity, t, :], bank[t][0:rows, 0:ROW], ACT.Copy,
                                         scale=rstd[0:rows, parity, t:t + 1]).then_inc(s_xt_out, 1)

            def store(s, parity):
                if not exists(s):
                    return
                tiles, rows, _ = shape(s)
                act.wait_ge(s_xt_out, tiles_before(s) + tiles)
                act.dma_start(tokens_of(table, s), xt_out[0:rows, parity, 0:tiles, :]).then_inc(s_table[parity], 16)
                act.dma_start(tokens_of(al_table, s), xt_out[0:rows, parity, 0:tiles, D + H:ROW]).then_inc(s_table[parity], 16)

            assert FULL - SPLIT_HI == E
            steps(act, SPLIT_HI, a_step)
            store(FULL - 1, (FULL - 1) % 2)
            xt_rows(FULL, FULL % 2, None)
            store(FULL, FULL % 2)

            def b_exp(s):
                tiles, rows, _ = shape(s)
                act.wait_ge(s_score, s + 1)
                nc.scalar.activation(expo[0:rows, 0:tiles, :], shifted[0:rows, 0:tiles, :], ACT.Exp).then_inc(s_exp, 1)

            def b_split(s, parity):
                _, _, n = shape(s)
                act.wait_ge(s_b_tr, s + 1)
                at_least(act, s_h, (s - 1) * E * HALVES)
                for k in range(KT):
                    last = nc.scalar.activation(x2T_hi[:, parity, k, 0:n], bank[6 + k][:, 0:n], ACT.Copy, scale=SPLIT)
                last.then_inc(s_x2T_hi, 1)

            def b_logit_exp(s):
                tiles, rows, _ = shape(s)
                act.wait_ge(s_lshift, s + 1)
                nc.scalar.activation(logit_exp[0:rows, 0:tiles, :], logit_shifted[0:rows, 0:tiles, :],
                                     ACT.Exp).then_inc(s_lexp, 1)

            def exponentials(s):
                if exists(s - 1):
                    b_logit_exp(s - 1)
                if exists(s):
                    b_exp(s)

            def b_combT(s, parity):
                _, _, n = shape(s)
                act.wait_ge(s_comb_tr, s + 1)
                if exists(s - 1):
                    act.wait_ge(s_y, item_done(s - 1, E))
                nc.scalar.copy(combT[:, parity, 0:n], bank[7][:].bitcast(fp16)[0:96, 0:n]).then_inc(s_combT, 1)

            def hidden(c, e):
                _, _, n = shape(c)
                q = c * E + e
                for f in range(HALVES):
                    act.wait_ge(s_h, q * HALVES + f + 1)
                    at_least(act, s_hlo, (q - 1) * HALVES)
                    nc.scalar.activation(h32[:, e % 2, f, 0:n], bank[2 * (e % 2) + f][:, 0:n], ACT.Gelu,
                                         bias=b1_col[:, e * HALVES + f:e * HALVES + f + 1],
                                         scale=UNSPLIT).then_inc(s_gelu, 1)
                pc, pe = before(c, e, RING_H)
                if exists(pc):
                    act.wait_ge(s_y, item_done(pc, pe))
                for f in range(HALVES):
                    act.wait_ge(s_gelu, q * HALVES + f + 1)
                    nc.scalar.activation(h_hi[:, e % RING_H, f, 0:n], h32[:, e % 2, f, 0:n], ACT.Copy,
                                         scale=H_SPLIT).then_inc(s_hhi, 1)

            def c_step(s, parity, i=None):
                c = s - 1
                for e in range(E):
                    if e == 0 and i is None and s == 1:
                        exponentials(s)
                    if exists(c):
                        hidden(c, e)
                    if e == 0 and not (i is None and s == 1):
                        exponentials(s)
                    if e == 3 and exists(c):
                        b_combT(c, 1 - parity)
                    if e == 6 and exists(s):
                        b_split(s, parity)

            steps(act, 4, c_step, 1)

        @block.vector
        def _(dve):
            link = Chain(dve, setup_chain, 0)

            def attention_columns():
                dve.wait_ge(s_w, 48)
                for n in range(2):
                    link(nc.vector.tensor_tensor(attn_prod[:], wext[:, :, 0:D].rearrange("p k (h c) -> p k h c", h=H),
                                                 attn[:, n, :, :].unsqueeze(1).to_broadcast([P, KT, H, C]), ALU.mult))
                    link(nc.vector.tensor_reduce(wext[:, :, D + n * H:D + (n + 1) * H], attn_prod[:], X, ALU.add))
                dve.sem_inc(s_wext, 1)

            def small_inputs():
                dve.wait_ge(s_small, 16 * 9)
                nc.vector.memset(rows_f[:], 0.0)
                link(nc.vector.memset(b2_parts[:], 0.0))
                for n in range(2):
                    nc.vector.tensor_copy(rows_f[0:TILES, n, 0:TAIL_ROWS], rows_in[0:TILES, n, 0:TAIL_ROWS])
                    nc.vector.tensor_copy(rows_f[0:TILES - 1, n, TAIL_ROWS:P], rows_in[0:TILES - 1, n, TAIL_ROWS:P])
                link(nc.vector.memset(b2_hi[:], 0.0))
                dve.sem_inc(s_rows_f, 1)
                for row in (0, 32, 64):
                    last = nc.vector.tensor_scalar(b2_hi[row:row + E, :], b2_in[row:row + E, :], SPLIT, None, ALU.mult)
                link(last)
                for row in (0, 64):
                    nc.vector.tensor_copy(b2_parts[row:row + E, :], b2_hi[row:row + E, :])
                link(nc.vector.scalar_tensor_tensor(out=b2_parts[32:32 + E, :], in0=b2_in[32:32 + E, :], scalar=SPLIT,
                                                    in1=b2_hi[32:32 + E, :], op0=ALU.mult, op1=ALU.subtract))

            def transposed_inputs():
                dve.wait_ge(s_setup_tr, 1)
                nc.vector.tensor_scalar(router64[:], bank[7][:, 0:KT * E].rearrange("p (k e) -> p k e", k=KT), SPLIT, None, ALU.mult)
                nc.vector.tensor_copy(b1_col[:], bank[7][:, 16:16 + E * HALVES])
                link(nc.vector.tensor_copy(index[:], bank[7][:, 64:64 + 2 * TILES].rearrange("p (n t) -> p n t", n=2)))
                link(nc.vector.tensor_copy(router_hi[:], router64[:]))
                nc.vector.tensor_tensor(router_lo[:], router64[:], router_hi[:], ALU.subtract).then_inc(s_setup, 1)

            def norm_stats(link, rows, tiles, v, get):
                settle(dve)
                for t in range(tiles):
                    last = nc.vector.bn_stats(stats[0:rows, t, :], get(t))
                link(last)
                settle(dve)
                for t in range(tiles):
                    last = nc.vector.bn_aggr(mean_var[0:rows, v, t, :], stats[0:rows, t, :])
                link(last)
                return nc.vector.tensor_scalar(var_eps[0:rows, v, 0:tiles], mean_var[0:rows, v, 0:tiles, 1], EPS, None, ALU.add)

            def norm_rstd(link, rows, tiles, v):
                r, n = rstd_0[0:rows, v, 0:tiles], newton[0:rows, v, 0:tiles]
                link(nc.vector.tensor_tensor(n, r, r, ALU.mult))
                link(nc.vector.tensor_tensor(n, n, var_eps[0:rows, v, 0:tiles], ALU.mult))
                link(nc.vector.tensor_scalar(n, n, -0.5, 1.5, ALU.mult, ALU.add))
                return nc.vector.tensor_tensor(rstd[0:rows, v, 0:tiles], r, n, ALU.mult)

            link_a = Chain(dve, a_chain, 2)
            link_r = Chain(dve, a_rstd_chain, 3)

            def a_step(s, parity, i=None):
                if exists(s):
                    a_stats(s, parity, i)
                if i is None and s == 1:
                    attention_columns()
                if exists(s - 1):
                    a_rstd(s - 1, 1 - parity)
                if i is None and s == FULL:
                    small_inputs()
                if i is None and s == FULL + 1:
                    transposed_inputs()
                if i is not None or s >= SPLIT_LO:
                    split_expert(s - SPLIT_LO)

            def a_stats(s, parity, i):
                tiles, rows, _ = shape(s)
                link_a.step(s)
                dve.wait_ge(s_x[parity], nth(s, parity, i) * 16 + 16)
                at_least(dve, s_x0, s - 1)
                xs = x_of(s)
                norm_stats(link_a, rows, tiles, parity, lambda t: xs[:, t, :]).then_inc(s_a_var, 1)

            def a_rstd(s, parity):
                tiles, rows, _ = shape(s)
                link_r.step(s)
                dve.wait_ge(s_a_pow, s + 1)
                if exists(s - 2):
                    dve.wait_ge(s_xt_out, tiles_before(s - 1))
                norm_rstd(link_r, rows, tiles, parity).then_inc(s_a_rstd, 1)

            def split_expert(e):
                dve.wait_ge(s_split_hi, e + 1)
                settle(dve)
                for n in range(2):
                    w, hi, lo = (a[n][:, bass.ds(e, 1), :, :] for a in (w_in, w_hi, w_lo))
                    last = nc.vector.scalar_tensor_tensor(out=lo, in0=w, scalar=SPLIT, in1=hi, op0=ALU.mult, op1=ALU.subtract)
                last.then_inc(s_experts_split, 1)

            assert FULL + 2 - SPLIT_LO == E
            steps(dve, SPLIT_LO, a_step, 1)
            dve.wait_ge(s_const, 6)

            link_b = Chain(dve, b_chain, 11)
            link_b2 = Chain(dve, b2_chain, 16)

            def b_scores(s, parity, i):
                tiles, rows, _ = shape(s)
                link_b.step(s)
                sl = (slice(0, rows), slice(0, tiles))
                earlier = nth(s, parity, i) * GT - (0 if parity or is_tail(s) else GT - 1)
                dve.wait_ge(s_gather[parity], 32 * (earlier + tiles))
                link_b(nc.vector.tensor_tensor(score[sl], xg[0:rows, parity, 0:tiles, D:D + H],
                                               alg[0:rows, parity, 0:tiles, :], ALU.add))
                link_b(nc.vector.scalar_tensor_tensor(out=lrelu[sl], in0=score[sl], scalar=SLOPE, in1=score[sl],
                                                      op0=ALU.mult, op1=ALU.max))
                link_b(nc.vector.tensor_reduce(top[sl], lrelu[sl], X, ALU.max))
                nc.vector.tensor_tensor(shifted[sl], lrelu[sl], top[sl].unsqueeze(2).to_broadcast([rows, tiles, H]),
                                        ALU.subtract).then_inc(s_score, 1)

            def b_alpha(s):
                tiles, rows, _ = shape(s)
                sl = (slice(0, rows), slice(0, tiles))
                dve.wait_ge(s_exp, s + 1)
                link_b(nc.vector.tensor_reduce(total[sl], expo[sl], X, ALU.add))
                link_b(nc.vector.reciprocal(inverse[sl], total[sl]))
                nc.vector.tensor_tensor(alpha[sl], expo[sl], inverse[sl].unsqueeze(2).to_broadcast([rows, tiles, H]),
                                        ALU.mult).then_inc(s_alpha, 1)

            def b_message(s, parity):
                tiles, rows, _ = shape(s)
                sl = (slice(0, rows), slice(0, tiles))
                if by_vector(s):
                    dve.wait_ge(s_alpha, s + 1)
                    weighted_rows(nc.vector, s, parity).then_inc(s_prod, 1)
                dve.wait_ge(s_prod, s + 1)
                nc.vector.tensor_reduce(tmp[sl], prod[sl].rearrange("p t h c -> p t c h"), X, ALU.add).then_inc(s_tmp, 1)
                if by_vector(s):
                    dve.wait_ge(s_tmp, s + 1)
                    add_message(nc.vector, s).then_inc(s_x1, 1)

            def b_stats(s):
                tiles, rows, _ = shape(s)
                xs = x_of(s)
                dve.wait_ge(s_x1, s + 1)
                norm_stats(link_b, rows, tiles, 0, lambda t: xs[:, t, :]).then_inc(s_b_var, 1)

            def b_norm(s):
                tiles, rows, _ = shape(s)
                xs = x_of(s)
                dve.wait_ge(s_b_pow, s + 1)
                link_b(norm_rstd(link_b, rows, tiles, 0))
                at_least(dve, s_b_tr, s)
                at_least(dve, s_acc0, s)
                for t in range(tiles):
                    last = nc.vector.tensor_scalar(x2[0:rows, t, :], xs[:, t, :], mean_var[0:rows, 0, t, 0:1],
                                                   rstd[0:rows, 0, t:t + 1], ALU.subtract, ALU.mult)
                last.then_inc(s_x2, 1)

            def b_split(s, parity):
                tiles, rows, n = shape(s)
                dve.wait_ge(s_x2T_hi, s + 1)
                for k in range(KT):
                    last = nc.vector.scalar_tensor_tensor(out=x2T_lo[:, parity, k, 0:n], in0=bank[6 + k][:, 0:n], scalar=SPLIT,
                                                          in1=x2T_hi[:, parity, k, 0:n], op0=ALU.mult, op1=ALU.subtract)
                last.then_inc(s_x2T_lo, 1)

            def b_logits(s):
                tiles, rows, _ = shape(s)
                sl = (slice(0, rows), slice(0, tiles))
                link_b2.step(s)
                dve.wait_ge(s_logits, s + 1)
                link_b2(nc.vector.tensor_scalar(logits[sl], bank[6][0:rows, 0:tiles * E].rearrange("p (t e) -> p t e", e=E),
                                                UNSPLIT, None, ALU.mult))
                link_b2(nc.vector.tensor_reduce(logit_top[sl], logits[sl], X, ALU.max))
                nc.vector.tensor_tensor(logit_shifted[sl], logits[sl], logit_top[sl].unsqueeze(2).to_broadcast([rows, tiles, E]),
                                        ALU.subtract).then_inc(s_lshift, 1)

            def b_best(s):
                tiles, rows, _ = shape(s)
                sl = (slice(0, rows), slice(0, tiles))
                wide = [rows, tiles, E]
                dve.wait_ge(s_lexp, s + 1)
                link_b2(nc.vector.tensor_reduce(prob_total[sl], logit_exp[sl], X, ALU.add))
                link_b2(nc.vector.reciprocal(prob_inverse[sl], prob_total[sl]))
                link_b2(nc.vector.tensor_tensor(prob[sl], logit_exp[sl], prob_inverse[sl].unsqueeze(2).to_broadcast(wide), ALU.mult))
                settle(dve)
                for t in range(tiles):
                    last = nc.vector.max(best[0:rows, t, :], prob[0:rows, t, :])
                link_b2(last)
                settle(dve)
                for t in range(tiles):
                    last = nc.vector.max_index(best_index[0:rows, t, :], best[0:rows, t, :], prob[0:rows, t, :])
                link_b2(last)

            def b_route(s, parity):
                tiles, rows, _ = shape(s)
                sl = (slice(0, rows), slice(0, tiles))
                wide = [rows, tiles, E]
                link_b2(nc.vector.tensor_copy(best_f[sl], best_index[0:rows, 0:tiles, 0:TOP_K]))
                for n in range(TOP_K):
                    last = nc.vector.tensor_tensor(mask[0:rows, n, 0:tiles, :], iota8[0:rows].unsqueeze(1).to_broadcast(wide),
                                                   best_f[0:rows, 0:tiles, n:n + 1].to_broadcast(wide), ALU.is_equal)
                link_b2(last)
                link_b2(nc.vector.tensor_tensor(mask[0:rows, 0, 0:tiles, :], mask[0:rows, 0, 0:tiles, :],
                                                mask[0:rows, 1, 0:tiles, :], ALU.add))
                link_b2(nc.vector.tensor_tensor(kept[sl], mask[0:rows, 0, 0:tiles, :], prob[sl], ALU.mult))
                link_b2(nc.vector.tensor_reduce(prob_total[sl], kept[sl], X, ALU.add))
                link_b2(nc.vector.tensor_scalar(prob_total[sl], prob_total[sl], 1e-12, None, ALU.max))
                link_b2(nc.vector.reciprocal(prob_inverse[sl], prob_total[sl]))
                link_b2(nc.vector.scalar_tensor_tensor(out=comb64[sl], in0=kept[sl], scalar=SPLIT,
                                                       in1=prob_inverse[sl].unsqueeze(2).to_broadcast(wide),
                                                       op0=ALU.mult, op1=ALU.mult))
                at_least(dve, s_comb_tr, s)
                nc.vector.tensor_copy(comb_parts[0:rows, 0:tiles, 0:E], comb64[sl])
                nc.vector.tensor_copy(comb_parts[0:rows, 0:tiles, 32:32 + E], comb64[sl])
                link_b2(nc.vector.tensor_scalar(comb[0:rows, parity, 0:tiles, :], comb64[sl], H_UNSPLIT / SPLIT, None, ALU.mult))
                nc.vector.tensor_tensor(comb_parts[0:rows, 0:tiles, 64:64 + E], comb64[sl], comb_parts[0:rows, 0:tiles, 0:E],
                                        ALU.subtract).then_inc(s_comb, 1)

            def remainder(c, e):
                _, _, n = shape(c)
                q = c * E + e
                for f in range(HALVES):
                    dve.wait_ge(s_hhi, q * HALVES + f + 1)
                    nc.vector.scalar_tensor_tensor(out=h_lo[:, e % RING_H, f, 0:n], in0=h32[:, e % 2, f, 0:n], scalar=H_SPLIT,
                                                   in1=h_hi[:, e % RING_H, f, 0:n], op0=ALU.mult,
                                                   op1=ALU.subtract).then_inc(s_hlo, 1)

            def accumulate(c, j, parity):
                tiles, rows, _ = shape(c)
                if j == 0:
                    dve.wait_ge(s_acc0, c + 1)
                for b in range(-(-tiles // 2)):
                    u = uses(c, j, b)
                    dve.wait_ge(s_y, u)
                    at_least(dve, s_acc, u - (1 if is_tail(c) else 2))
                    y = output_bank(c, j, b)
                    for t in range(2 * b, min(tiles, 2 * b + 2)):
                        a = acc[0:rows, parity, t, :]
                        weight_of = UNSPLIT if j == E else comb[0:rows, parity, t, j:j + 1]
                        last = nc.vector.scalar_tensor_tensor(out=a, in0=y[0:rows, (t % 2) * D:(t % 2 + 1) * D], scalar=weight_of,
                                                              in1=a, op0=ALU.mult, op1=ALU.add)
                    last.then_inc(s_acc, 1)

            def finish(c, e, parity):
                pc, pe = before(c, e, LAG)
                own = parity if e >= LAG else 1 - parity
                if exists(pc):
                    accumulate(pc, pe, own)
                    if pe == E - 1:
                        accumulate(pc, E, own)

            def c_step(s, parity, i=None):
                c = s - 1
                for e in range(E):
                    if exists(c):
                        if e == 0:
                            b_logits(c)
                        if e == 2:
                            b_route(c, 1 - parity)
                    if exists(s):
                        at = (0, 0, 0, 1, 3) if i is None and s == 1 else (0, 1, 3, 4, 5)
                        if e == at[0]:
                            b_scores(s, parity, i)
                        if e == at[1]:
                            b_alpha(s)
                        if e == at[2]:
                            b_message(s, parity)
                        if e == at[3]:
                            b_stats(s)
                        if e == at[4]:
                            b_norm(s)
                        if e == 7:
                            b_split(s, parity)
                    if exists(c):
                        if e == 1:
                            b_best(c)
                        remainder(c, e)
                        finish(c, e, 1 - parity)

            steps(dve, 4, c_step, 1)
            for e in range(LAG):
                finish(FULL + 1, e, (FULL + 1) % 2)

        @block.tensor
        def _(pe):
            pe.wait_ge(s_const, 6)

            def transposed_inputs():
                pe.wait_ge(s_small, 16 * 9)
                pe.wait_ge(s_rows_f, 1)
                for k in range(KT):
                    nc.tensor.transpose(bank[7][:, k * E:(k + 1) * E], router_in[:, k * P:(k + 1) * P], ident[0:E, 0:E])
                nc.tensor.transpose(bank[7][:, 16:16 + E * HALVES], b1_in[:], ident[0:E * HALVES, 0:E * HALVES])
                for n in range(2):
                    last = nc.tensor.transpose(bank[7][:, 64 + n * TILES:64 + (n + 1) * TILES], rows_f[:, n, :],
                                               ident[0:TILES, 0:TILES])
                last.then_inc(s_setup_tr, 1)

            def a_step(s, parity, i=None):
                tiles, rows, _ = shape(s)
                if i is None and s == 2:
                    xt_product(1, 1)
                pe.wait_ge(s_x0, s + 1)
                at_least(pe, s_x0T, s - 1)
                for k in range(KT):
                    for t in range(tiles):
                        last = nc.tensor.transpose(bank[4 + 2 * parity + k][:, t * P:t * P + rows],
                                                   x0[0:rows, parity, t, k * P:(k + 1) * P], ident[0:rows, 0:rows])
                last.then_inc(s_a_tr, 1)
                if i is None and s == 1:
                    pe.wait_ge(s_wext, 1)
                if not (i is None and s == 2):
                    xt_product(s - 1, 1 - parity)
                if i is None and s == FULL:
                    transposed_inputs()

            def xt_product(s, parity):
                if not exists(s):
                    return
                tiles, rows, _ = shape(s)
                pe.wait_ge(s_x0T, s + 1)
                for t in range(tiles):
                    if exists(s - 1) and t < shape(s - 1)[0]:
                        pe.wait_ge(s_xt_out, tiles_before(s - 1) + t + 1)
                    for k in range(KT):
                        last = nc.tensor.matmul(bank[t][0:rows, 0:ROW], x0T[:, parity, k, t * P:t * P + rows], wext[:, k, :],
                                                start=(k == 0), stop=(k == KT - 1))
                    last.then_inc(s_xt, 1)

            steps(pe, 4, a_step)
            xt_product(FULL, FULL % 2)

            def b_transpose(s):
                tiles, rows, _ = shape(s)
                pe.wait_ge(s_x2, s + 1)
                at_least(pe, s_lshift, s)
                at_least(pe, s_combT, s)
                for k in range(KT):
                    for t in range(tiles):
                        last = nc.tensor.transpose(bank[6 + k][:, t * P:t * P + rows], x2[0:rows, t, k * P:(k + 1) * P],
                                                   ident[0:rows, 0:rows])
                last.then_inc(s_b_tr, 1)

            def b_router(s, parity):
                tiles, rows, _ = shape(s)
                pe.wait_ge(s_x2T_lo, s + 1)
                for t in range(tiles):
                    parts = [(x, w, k) for k in range(KT)
                             for x, w in ((x2T_hi, router_hi), (x2T_hi, router_lo), (x2T_lo, router_hi))]
                    for n, (xp, wp, k) in enumerate(parts):
                        last = nc.tensor.matmul(bank[6][0:rows, t * E:(t + 1) * E], xp[:, parity, k, t * P:t * P + rows], wp[:, k, :],
                                                start=(n == 0), stop=(n == len(parts) - 1))
                last.then_inc(s_logits, 1)

            def b_combine(s):
                tiles, rows, _ = shape(s)
                pe.wait_ge(s_comb, s + 1)
                if exists(s - 1):
                    pe.wait_ge(s_acc, item_done(s - 1, E))
                for t in range(tiles):
                    last = nc.tensor.transpose(bank[7][:].bitcast(fp16)[0:96, t * P:t * P + rows], comb_parts[0:rows, t, :],
                                               ident16[0:rows, 0:rows])
                last.then_inc(s_comb_tr, 1)

            def first(c, e, parity):
                _, _, n = shape(c)
                q = c * E + e
                for f in range(HALVES):
                    at_least(pe, s_gelu, (q - 2) * HALVES + f + 1)
                    parts = [(w, x, k) for k in range(KT)
                             for w, x in ((w_hi[0], x2T_hi), (w_hi[0], x2T_lo), (w_lo[0], x2T_hi))]
                    for m, (wp, xp, k) in enumerate(parts):
                        last = nc.tensor.matmul(bank[2 * (e % 2) + f][:, 0:n], wp[:, e, k, f * P:(f + 1) * P],
                                                xp[:, parity, k, 0:n], start=(m == 0), stop=(m == len(parts) - 1))
                    last.then_inc(s_h, 1)

            def bias(c, parity):
                pe.wait_ge(s_combT, c + 1)
                pe.wait_ge(s_lshift, FULL + 1 if isinstance(c, int) and c == FULL else c + 2)
                output(c, E, lambda t, rows: [(combT[:, parity, t * P:t * P + rows], b2_parts[:])])

            def second(c, e):
                pe.wait_ge(s_hlo, (c * E + e + 1) * HALVES)
                r = e % RING_H
                output(c, e, lambda t, rows: [
                    (hp[:, r, f, t * P:t * P + rows], wp[:, e, f, :]) for f in range(HALVES)
                    for hp, wp in ((h_hi, w_hi[1]), (h_hi, w_lo[1]), (h_lo, w_hi[1]))])

            def output(c, j, parts_of):
                tiles, rows, _ = shape(c)
                for b in range(-(-tiles // 2)):
                    if j < E:
                        at_least(pe, s_acc, bank_added(c, j, b))
                    y = output_bank(c, j, b)
                    for t in range(2 * b, min(tiles, 2 * b + 2)):
                        parts = parts_of(t, rows)
                        for m, (lhsT, rhs) in enumerate(parts):
                            last = nc.tensor.matmul(y[0:rows, (t % 2) * D:(t % 2 + 1) * D], lhsT, rhs,
                                                    start=(m == 0), stop=(m == len(parts) - 1))
                    last.then_inc(s_y, 1)

            def seconds(c, e, parity):
                pc, pe_ = before(c, e, LAG)
                if exists(pc):
                    second(pc, pe_)
                    if pe_ == E - 1:
                        bias(pc, 1 - parity)

            pe.wait_ge(s_experts_split, E)

            def c_step(s, parity, i=None):
                c = s - 1
                for e in range(E):
                    if exists(c):
                        first(c, e, 1 - parity)
                        if e == 3:
                            b_combine(c)
                    if exists(s):
                        if e == 6:
                            b_transpose(s)
                        if e == 7:
                            b_router(s, parity)
                    if exists(c):
                        seconds(c, e, 1 - parity)

            steps(pe, 4, c_step, 1)
            for e in range(LAG):
                seconds(FULL + 1, e, (FULL + 1) % 2)


_INS = ['x', 'src', 'dst', 'L0_gnn_weight', 'L0_gnn_attn_l', 'L0_gnn_attn_r', 'L0_ffn_router_w', 'L0_ffn_w1',
        'L0_ffn_b1', 'L0_ffn_w2', 'L0_ffn_b2']
_OUTS = [((N, D), 'float32')]


def kernel(**inputs):
    import numpy as _np
    import concourse.bacc as _bacc
    from concourse import mybir as _mybir
    from concourse.bass_utils import run_bass_kernel_spmd as _run

    nc = _bacc.Bacc("TRN2", target_bir_lowering=False, num_devices=1)
    arrays, args = {}, []
    for name in _INS:
        a = _np.ascontiguousarray(inputs[name])
        arrays[f"in_{name}_dram"] = a
        args.append(nc.dram_tensor(f"in_{name}_dram", a.shape, _mybir.dt.from_np(a.dtype), kind="ExternalInput").ap())
    for i, (shape, dtype) in enumerate(_OUTS):
        dt = _mybir.dt.from_np(_np.dtype(dtype))
        args.append(nc.dram_tensor(f"out_{i}_dram", shape, dt, kind="ExternalOutput").ap())
    build(nc, *args)
    r = _run(nc, [arrays], core_ids=[0])
    got = tuple(r.results[0][f"out_{i}_dram"] for i in range(len(_OUTS)))
    return got[0]
```
